# Optimizing a Trainium2 kernel written in Bass

```python
import numpy as np
import jax
import jax.numpy as jnp

def _softmax(x, axis=-1):
    return jax.nn.softmax(x, axis=axis)

def _gelu(x):
    return jax.nn.gelu(x, approximate=True)

def _silu(x):
    return jax.nn.silu(x)

def _sigmoid(x):
    return jax.nn.sigmoid(x)

def _layernorm(x, axis=-1, eps=1e-05):
    m = jnp.mean(x, axis=axis, keepdims=True)
    v = jnp.var(x, axis=axis, keepdims=True)
    return (x - m) / jnp.sqrt(v + eps)

def _scatter_add(tgt, idx, src, axis=0):
    return tgt.at[idx].add(src)

def _segment_sum(src, seg, n):
    return jax.ops.segment_sum(src, seg, n)
kernel_name = 'mk_gnn_preln_d1_gnn_r8_428716'

def setup_inputs(seed: int=0):
    np.random.seed(seed)
    _w = jnp.asarray

    def _rec_inputs():
        import jax
        import jax.numpy as jnp
        _gk = jax.random.key(seed)
        x = -0.0001006 + 1 * jax.random.normal(jax.random.fold_in(_gk, 1), (12500, 96), jnp.float32)
        src = jax.random.randint(jax.random.fold_in(_gk, 2), (400000,), 0, 12500, jnp.int32)
        dst = jnp.minimum((12500 * jax.random.uniform(jax.random.fold_in(_gk, 3), (400000,)) ** 2.0).astype(jnp.int32), 99999)
        _o = jnp.argsort(dst, stable=True)
        src = src[_o]
        dst = dst[_o]
        edge_attr_16 = 0.000254156 + 0.999948 * jax.random.normal(jax.random.fold_in(_gk, 11), (400000, 16), jnp.float32)
        return (x, src, dst, edge_attr_16)
    x, src, dst, edge_attr_16 = _rec_inputs()

    def _L0_gnn_setup():
        import jax, jax.numpy as jnp
        import numpy as np
        NEG_SLOPE_ATT = 0.2
        NEG_SLOPE_ACT = 0.01
        EPS_GN = 1e-05

        def _leaky(x, s):
            return jnp.where(x >= 0, x, s * x)

        def _gat_conv(x, src, dst, W, a_src, a_dst, b, n_nodes):
            h = x @ W.T
            alpha_s = h @ a_src
            alpha_d = h @ a_dst
            e = _leaky(alpha_s[src] + alpha_d[dst], NEG_SLOPE_ATT)
            m = jax.ops.segment_max(e, dst, num_segments=n_nodes)
            ex = jnp.exp(e - m[dst])
            z = jax.ops.segment_sum(ex, dst, num_segments=n_nodes)
            alpha = ex / z[dst]
            msg = h[src] * alpha[:, None]
            out = jax.ops.segment_sum(msg, dst, num_segments=n_nodes) + b
            return out

        def _graph_norm(x, weight, bias, mean_scale):
            mean = jnp.mean(x, axis=0)
            xc = x - mean_scale * mean
            var = jnp.mean(xc * xc, axis=0)
            return weight * xc * jax.lax.rsqrt(var + EPS_GN) + bias
        key = jax.random.key(seed)
        ks = jax.random.split(key, 12)
        N, E, C, ED = (6250, 100000, 96, 16)
        sc = 1.0 / np.sqrt(C)
        inp = {'x': jax.random.normal(ks[0], (N, C), jnp.float32), 'edge_index': jax.random.randint(ks[1], (2, E), 0, N, jnp.int32), 'edge_attr': jax.random.normal(ks[2], (E, ED), jnp.float32), 'W1': jax.random.normal(ks[3], (C, C), jnp.float32) * sc, 'att_src1': jax.random.normal(ks[4], (C,), jnp.float32) * sc, 'att_dst1': jax.random.normal(ks[5], (C,), jnp.float32) * sc, 'b1': jnp.zeros((C,), jnp.float32), 'W2': jax.random.normal(ks[6], (C, C), jnp.float32) * sc, 'att_src2': jax.random.normal(ks[7], (C,), jnp.float32) * sc, 'att_dst2': jax.random.normal(ks[8], (C,), jnp.float32) * sc, 'b2': jnp.zeros((C,), jnp.float32), 'gn_weight': jnp.ones((C,), jnp.float32), 'gn_bias': jnp.zeros((C,), jnp.float32), 'gn_mean_scale': jnp.ones((C,), jnp.float32)}
        return inp
    _L0_gnn_all = _L0_gnn_setup()
    _L0_gnn_in = {k: v for k, v in _L0_gnn_all.items() if k in ('W1', 'att_src1', 'att_dst1', 'b1', 'W2', 'att_src2', 'att_dst2', 'b2', 'gn_weight', 'gn_bias', 'gn_mean_scale')}
    del _L0_gnn_all
    return {'x': x, 'src': src, 'dst': dst, 'edge_attr_16': edge_attr_16, 'L0_gnn_W1': _L0_gnn_in['W1'], 'L0_gnn_att_src1': _L0_gnn_in['att_src1'], 'L0_gnn_att_dst1': _L0_gnn_in['att_dst1'], 'L0_gnn_b1': _L0_gnn_in['b1'], 'L0_gnn_W2': _L0_gnn_in['W2'], 'L0_gnn_att_src2': _L0_gnn_in['att_src2'], 'L0_gnn_att_dst2': _L0_gnn_in['att_dst2'], 'L0_gnn_b2': _L0_gnn_in['b2'], 'L0_gnn_gn_weight': _L0_gnn_in['gn_weight'], 'L0_gnn_gn_bias': _L0_gnn_in['gn_bias'], 'L0_gnn_gn_mean_scale': _L0_gnn_in['gn_mean_scale']}

def reference(x, src, dst, edge_attr_16, L0_gnn_W1, L0_gnn_att_src1, L0_gnn_att_dst1, L0_gnn_b1, L0_gnn_W2, L0_gnn_att_src2, L0_gnn_att_dst2, L0_gnn_b2, L0_gnn_gn_weight, L0_gnn_gn_bias, L0_gnn_gn_mean_scale):
    import jax
    import jax.numpy as jnp

    def _L0_gnn_ref(x, edge_index, edge_attr, W1, att_src1, att_dst1, b1, W2, att_src2, att_dst2, b2, gn_weight, gn_bias, gn_mean_scale):
        import jax, jax.numpy as jnp
        import numpy as np
        NEG_SLOPE_ATT = 0.2
        NEG_SLOPE_ACT = 0.01
        EPS_GN = 1e-05

        def _leaky(x, s):
            return jnp.where(x >= 0, x, s * x)

        def _gat_conv(x, src, dst, W, a_src, a_dst, b, n_nodes):
            h = x @ W.T
            alpha_s = h @ a_src
            alpha_d = h @ a_dst
            e = _leaky(alpha_s[src] + alpha_d[dst], NEG_SLOPE_ATT)
            m = jax.ops.segment_max(e, dst, num_segments=n_nodes)
            ex = jnp.exp(e - m[dst])
            z = jax.ops.segment_sum(ex, dst, num_segments=n_nodes)
            alpha = ex / z[dst]
            msg = h[src] * alpha[:, None]
            out = jax.ops.segment_sum(msg, dst, num_segments=n_nodes) + b
            return out

        def _graph_norm(x, weight, bias, mean_scale):
            mean = jnp.mean(x, axis=0)
            xc = x - mean_scale * mean
            var = jnp.mean(xc * xc, axis=0)
            return weight * xc * jax.lax.rsqrt(var + EPS_GN) + bias
        N = x.shape[0]
        loops = jnp.arange(N, dtype=edge_index.dtype)
        src = jnp.concatenate([edge_index[0], loops])
        dst = jnp.concatenate([edge_index[1], loops])
        residual = x
        h = _gat_conv(x, src, dst, W1, att_src1, att_dst1, b1, N)
        h = _leaky(_graph_norm(h, gn_weight, gn_bias, gn_mean_scale), NEG_SLOPE_ACT)
        h = _gat_conv(h, src, dst, W2, att_src2, att_dst2, b2, N)
        h = _graph_norm(h, gn_weight, gn_bias, gn_mean_scale)
        return _leaky(h + residual, NEG_SLOPE_ACT)
    edge_index = jnp.stack([src, dst])
    h = jnp.maximum(_layernorm(x, axis=-1), 0.0)
    x = x + _L0_gnn_ref(h, edge_index, edge_attr_16, L0_gnn_W1, L0_gnn_att_src1, L0_gnn_att_dst1, L0_gnn_b1, L0_gnn_W2, L0_gnn_att_src2, L0_gnn_att_dst2, L0_gnn_b2, L0_gnn_gn_weight, L0_gnn_gn_bias, L0_gnn_gn_mean_scale)
    return x

_drawn_inputs = setup_inputs


def setup_inputs(seed=0):
    import zlib

    import numpy as np

    out = dict(_drawn_inputs(seed))
    spreads = {'L0_gnn_b1': (0.0, 0.1),
     'L0_gnn_b2': (0.0, 0.1),
     'L0_gnn_gn_weight': (1.0, 0.2),
     'L0_gnn_gn_bias': (0.0, 0.1),
     'L0_gnn_gn_mean_scale': (1.0, 0.2)}
    factors = {}
    for name, (base, spread) in spreads.items():
        noise = np.random.default_rng([zlib.crc32(name.encode()), seed]).standard_normal(out[name].shape)
        drawn = base * np.exp(spread * noise) if base else spread * noise
        out[name] = jnp.asarray(drawn.astype(out[name].dtype))
    for name, factor in factors.items():
        out[name] = (out[name] * factor).astype(out[name].dtype)
    return out
```

```python
from contextlib import ExitStack

import concourse.bass as bass
from concourse import mybir

P = 128
C = 96
BLOCK = 125
BPW = 4
WIN = BLOCK * BPW
TAB = C + 2
EXT = C + 3
STATE = C + 3
SLOPE_ATT = 0.2
SLOPE_ACT = 0.01
EPS = 1e-5
BIG = 1e30

ALU = mybir.AluOpType
ACT = mybir.ActivationFunctionType
F32 = mybir.dt.float32
I32 = mybir.dt.int32
AX = mybir.AxisListType.X


class Chain:

    def __init__(self, eng, sem):
        self.eng, self.sem, self.n, self.turn = eng, sem, 0, 0

    def link(self, ins):
        ins.then_inc(self.sem, 1)
        self.n += 1
        self.eng.wait_ge(self.sem, self.turn + self.n)

    def enter(self, i, per):
        self.turn, self.first, self.per = i * per, self.n, per

    def leave(self, count):
        assert self.n - self.first == self.per, (self.n - self.first, self.per)
        self.turn, self.n = 0, self.first + self.per * count


def gat_kernel(nc, x, src, dst, W1, as1, ad1, b1, W2, as2, ad2, b2, gn_w, gn_b, gn_ms, out):
    N = x.shape[0]
    E = src.shape[0]
    NW = N // WIN
    TILES = E // P
    assert N % WIN == 0 and E % P == 0 and x.shape[1] == C

    with ExitStack() as ctx:
        def sb(name, shape, dt=F32):
            return ctx.enter_context(nc.sbuf_tensor(name, shape, dt))

        def ps(name, shape):
            return ctx.enter_context(nc.psum_tensor(name, shape, F32))

        def sem(name):
            return ctx.enter_context(nc.semaphore(name))

        def dram(name, shape, dt=F32):
            return nc.dram_tensor(name, shape, dt, kind="Internal").ap()

        table = dram("table", [N, TAB])
        alphas = dram("alphas", [N, 2])
        state = dram("state", [N, STATE])
        h0t = dram("h0t", [C, N])

        acc = sb("acc", [P, N])
        ht = sb("ht", [P, N])
        ident = sb("ident", [P, P])
        ones = sb("ones", [P, P])
        lower = sb("lower", [P, P])
        sel_delta = sb("sel_delta", [P, P])
        sel_z = sb("sel_z", [P, P])
        wraw = sb("wraw", [P, 2, C])
        avec = sb("avec", [P, 4])
        wext = sb("wext", [P, 2, EXT])
        gn = sb("gn", [P, 5])
        stat = sb("stat", [P, 8])
        xin = sb("xin", [P, BPW, C])
        xc = sb("xc", [P, BPW, C])
        xn = sb("xn", [P, BPW, C])
        xs = sb("xs", [P, 4, BPW])
        Y = sb("Y", [P, WIN])
        tabs = sb("tabs", [P, BPW, EXT])
        lin = sb("lin", [P, WIN])
        res = sb("res", [P, WIN])
        g_src = sb("g_src", [P, 1], I32)
        g_dst = sb("g_dst", [P, 1], I32)
        g_dstrow = sb("g_dstrow", [P, P], I32)
        g_sidx = sb("g_sidx", [P, 1], I32)
        g_rows = sb("g_rows", [P, TAB])
        g_old = sb("g_old", [P, STATE])
        g_new = sb("g_new", [P, STATE])
        g_eq = sb("g_eq", [P, P])
        g_tmp = sb("g_tmp", [P, P])
        g_diag = sb("g_diag", [P, P])
        g_w = sb("g_w", [P, TAB])
        g_c = sb("g_c", [P, 8])
        g_init = sb("g_init", [P, BPW, STATE])
        g_alph = sb("g_alph", [P, BPW, 2])

        psT = ps("psT", [P, 512])
        psH = ps("psH", [P, 512])
        psTab = ps("psTab", [P, 512])
        psD = ps("psD", [P, 512])
        psZ = ps("psZ", [P, 512])
        psE = ps("psE", [P, 512])
        psU = ps("psU", [P, 512])

        names = """weights_in consts_made own_vector own_scalar own_pool pool_passed sp_passed ext_made wt_psum wt_copied x_in xn_ready xt_done var_ready
        std_ready y_ready projected h_copied table_written h0_stored
        delta_spread self_weight total_ready z_spread norm_ready sum_ready shift_ready square_ready gn_std
        gn_ready lin_ready res_in v_ready v_back out_ready out_written
"""
        s = {k: sem(k) for k in names.split()}
        edge_names = """gi_in gi_ready gi_written e_src e_dst e_dstrow e_rows e_old e_new e_scattered e_diag e_row e_wt e_exp e_weighted e_sum
        gb_in gb_ready gb_turned gb_copied"""
        g = [{k: sem(f"{k}_{l}") for k in edge_names.split()} for l in range(2)]

        def x_window(w):
            return x[bass.ds(w * WIN, WIN), :].rearrange("(b p) c -> p b c", p=BLOCK)

        block = ctx.enter_context(nc.Block())

        @block.sync
        def _(sp):
            for i, (dst_ap, src_ap) in enumerate((
                    (wraw[0:C, 0, :], W1), (wraw[0:C, 1, :], W2),
                    (avec[0:C, 0:1], as1.rearrange("(c a) -> c a", a=1)), (avec[0:C, 1:2], ad1.rearrange("(c a) -> c a", a=1)),
                    (avec[0:C, 2:3], as2.rearrange("(c a) -> c a", a=1)), (avec[0:C, 3:4], ad2.rearrange("(c a) -> c a", a=1)),
                    (gn[0:C, 0:1], b1.rearrange("(c a) -> c a", a=1)), (gn[0:C, 1:2], b2.rearrange("(c a) -> c a", a=1)),
                    (gn[0:C, 2:3], gn_w.rearrange("(c a) -> c a", a=1)), (gn[0:C, 3:4], gn_b.rearrange("(c a) -> c a", a=1)),
                    (gn[0:C, 4:5], gn_ms.rearrange("(c a) -> c a", a=1)))):
                sp.dma_start(dst_ap, src_ap).then_inc(s["weights_in"], 16)

            def write_table(l, w):
                turn = l * NW + w
                sp.wait_ge(s["h_copied"], 2 * turn + 2)
                sp.dma_start(table[bass.ds(w * WIN, WIN), :].rearrange("(b p) c -> p b c", p=BLOCK),
                             tabs[0:BLOCK, :, 0:TAB]).then_inc(s["table_written"], 16)
                sp.dma_start(alphas[bass.ds(w * WIN, WIN), :].rearrange("(b p) c -> p b c", p=BLOCK),
                             tabs[0:BLOCK, :, C + 1:EXT]).then_inc(s["table_written"], 16)

            def general(l):
                sp.wait_ge(s["table_written"], 32 * NW * (l + 1))
                with sp.Fori(0, NW) as w:
                    turn = w
                    sp.wait_ge(g[l]["gi_written"], 16 * turn)
                    sp.dma_start(g_init[0:BLOCK, :, 0:TAB], table[bass.ds(w * WIN, WIN), :].rearrange("(b p) c -> p b c", p=BLOCK)).then_inc(g[l]["gi_in"], 16)
                    sp.dma_start(g_alph[0:BLOCK, :, :], alphas[bass.ds(w * WIN, WIN), :].rearrange("(b p) c -> p b c", p=BLOCK)).then_inc(g[l]["gi_in"], 16)
                    sp.wait_ge(g[l]["gi_ready"], turn + 1)
                    sp.dma_start(state[bass.ds(w * WIN, WIN), :].rearrange("(b p) c -> p b c", p=BLOCK), g_init[0:BLOCK, :, :]).then_inc(g[l]["gi_written"], 16)
                with sp.Fori(0, TILES) as t:
                    sp.wait_ge(g[l]["e_scattered"], 16 * t)
                    sp.dma_start(g_src[:, :], src[bass.ds(t * P, P)].rearrange("(p a) -> p a", a=1)).then_inc(g[l]["e_src"], 16)
                    sp.dma_start(g_dst[:, :], dst[bass.ds(t * P, P)].rearrange("(p a) -> p a", a=1)).then_inc(g[l]["e_dst"], 16)
                    sp.dma_start(g_dstrow[:, :], dst[bass.ds(t * P, P)].rearrange("(a p) -> a p", a=1).to_broadcast([P, P])).then_inc(g[l]["e_dstrow"], 16)
                sp.wait_ge(g[l]["e_scattered"], 16 * TILES)
                with sp.Fori(0, NW) as w:
                    turn = w
                    sp.wait_ge(g[l]["gb_turned"], turn)
                    sp.dma_start(g_init[0:BLOCK, :, :], state[bass.ds(w * WIN, WIN), :].rearrange("(b p) c -> p b c", p=BLOCK)).then_inc(g[l]["gb_in"], 16)

            with sp.Fori(0, NW) as w:
                sp.wait_ge(s["xn_ready"], w)
                sp.dma_start(xin[0:BLOCK, :, :], x_window(w)).then_inc(s["x_in"], 16)
                sp.wait_ge(s["y_ready"], w + 1)
                sp.sem_inc(s["sp_passed"], 1)
                sp.dma_start(h0t[:, bass.ds(w * WIN, WIN)], Y[0:C, :]).then_inc(s["h0_stored"], 16)
                write_table(0, w)
            general(0)
            with sp.Fori(0, NW) as w:
                write_table(1, w)
            general(1)
            sp.wait_ge(s["gn_ready"], 2)
            with sp.Fori(0, NW) as w:
                sp.wait_ge(s["v_ready"], w)
                sp.dma_start(res[0:C, :], h0t[:, bass.ds(w * WIN, WIN)]).then_inc(s["res_in"], 16)
                sp.wait_ge(s["out_ready"], w)
                sp.dma_start(xin[0:BLOCK, :, :], x_window(w)).then_inc(s["x_in"], 16)
                sp.wait_ge(s["out_ready"], w + 1)
                sp.dma_start(out[bass.ds(w * WIN, WIN), :].rearrange("(b p) c -> p b c", p=BLOCK), xn[0:BLOCK, :, :]).then_inc(s["out_written"], 16)
            sp.wait_ge(s["out_written"], 16 * NW)

        @block.gpsimd
        def _(pool):
            made = Chain(pool, s["own_pool"])
            made.link(pool.memset(ident[:, :], 0.0))
            made.link(pool.memset(ones[:, :], 1.0))
            made.link(pool.memset(sel_delta[:, :], 0.0))
            made.link(pool.memset(sel_z[:, :], 0.0))
            made.link(pool.affine_select(out=ident[:, :], in_=ident[:, :], compare_op=ALU.not_equal, fill=1.0, base=0,
                                         pattern=[[-1, P]], channel_multiplier=1))
            made.link(pool.affine_select(out=lower[:, :], in_=ones[:, :], compare_op=ALU.is_gt, fill=0.0, base=0,
                                         pattern=[[-1, P]], channel_multiplier=1))
            made.link(pool.affine_select(out=sel_delta[:, :], in_=sel_delta[:, :], compare_op=ALU.not_equal, fill=1.0,
                                         base=-(C + 1), pattern=[[0, P]], channel_multiplier=1))
            made.link(pool.affine_select(out=sel_z[:, :], in_=sel_z[:, :], compare_op=ALU.not_equal, fill=1.0,
                                         base=-C, pattern=[[0, P]], channel_multiplier=1))
            made.link(pool.memset(wext[:, :, :], 0.0))
            made.link(pool.memset(wext[C:C + 1, :, C:C + 1], 1.0))
            pool.memset(Y[C:C + 1, :], 1.0).then_inc(s["consts_made"], 1)

            last_node = pool.to_reg(N - 1)

            def general(l):
                pool.wait_ge(g[l]["gi_written"], 16 * NW)
                with pool.Fori(0, TILES) as t:
                    pool.wait_ge(g[l]["e_src"], 16 * t + 16)
                    pool.wait_ge(g[l]["e_dst"], 16 * t + 16)
                    pool.wait_ge(g[l]["e_scattered"], 16 * t)
                    pool.sem_inc(s["pool_passed"], 1)
                    pool.indirect_dma_start(g_rows[:, :], None, table, bass.IndirectOffsetOnAxis(ap=g_src[:, 0:1], axis=0)).then_inc(g[l]["e_rows"], 16)
                    pool.indirect_dma_start(g_old[:, :], None, state, bass.IndirectOffsetOnAxis(ap=g_dst[:, 0:1], axis=0)).then_inc(g[l]["e_old"], 16)
                    pool.wait_ge(g[l]["e_new"], t + 1)
                    pool.sem_inc(s["pool_passed"], 1)
                    pool.indirect_dma_start(state, bass.IndirectOffsetOnAxis(ap=g_sidx[:, 0:1], axis=0), g_new[:, :], None,
                                            bounds_check=last_node, oob_is_err=False).then_inc(g[l]["e_scattered"], 16)
                pool.wait_ge(g[l]["e_scattered"], 16 * TILES)

            general(0)
            general(1)

        @block.scalar
        def _(act):
            def copy_projection(l, w):
                turn = l * NW + w
                act.wait_ge(s["projected"], turn + 1)
                act.activation(ht[0:C + 1, bass.ds(w * WIN, WIN)], psH[0:C + 1, 0:WIN], ACT.Copy).then_inc(s["h_copied"], 1)
                act.wait_ge(s["table_written"], 32 * turn)
                act.activation(tabs[0:BLOCK, :, :], psTab[0:BLOCK, 0:BPW * EXT].rearrange("p (b c) -> p b c", b=BPW), ACT.Copy).then_inc(s["h_copied"], 1)

            def general(l):
                with act.Fori(0, TILES) as t:
                    act.wait_ge(g[l]["e_wt"], t + 1)
                    act.activation(g_c[:, 4:6], g_c[:, 2:4], ACT.Exp).then_inc(g[l]["e_exp"], 1)
                with act.Fori(0, NW) as w:
                    act.wait_ge(g[l]["gb_turned"], w + 1)
                    act.activation(acc[0:STATE, bass.ds(w * WIN, WIN)], psT[0:STATE, 0:WIN], ACT.Copy).then_inc(g[l]["gb_copied"], 1)

            def finish(l):
                with act.Fori(0, NW) as w:
                    turn = w + l * NW
                    act.wait_ge(s["delta_spread"], turn + 1)
                    act.wait_ge(s["total_ready"], turn)
                    act.activation(lin[0:C + 1, :], psD[0:C + 1, 0:WIN], ACT.Exp, scale=-1.0).then_inc(s["self_weight"], 1)
                act.wait_ge(s["norm_ready"], NW * (l + 1))
                act.activation(acc[0:C, :], acc[0:C, :], ACT.Identity, bias=gn[0:C, l:l + 1], accum_out=stat[0:C, 0:1]).then_inc(s["sum_ready"], 1)
                act.wait_ge(s["shift_ready"], l + 1)
                act.activation(ht[0:C, :], acc[0:C, :], ACT.Square, bias=stat[0:C, 1:2], accum_out=stat[0:C, 2:3]).then_inc(s["square_ready"], 1)
                act.wait_ge(s["var_ready"], NW + l + 1)
                act.activation(stat[0:C, 4:5], stat[0:C, 3:4], ACT.Sqrt).then_inc(s["gn_std"], 1)
                act.wait_ge(s["gn_ready"], l + 1)

            act.wait_ge(s["wt_psum"], 2)
            for l in range(2):
                act.activation(wext[0:C, l, 0:C], psT[0:C, l * C:(l + 1) * C], ACT.Copy).then_inc(s["wt_copied"], 1)
                act.activation(wext[0:C, l, C + 1:EXT], psT[0:C, 2 * C + 2 * l:2 * C + 2 * l + 2], ACT.Copy).then_inc(s["wt_copied"], 1)
            with act.Fori(0, NW) as w:
                act.wait_ge(s["var_ready"], w + 1)
                act.activation(xs[0:BLOCK, 2, :], xs[0:BLOCK, 1, :], ACT.Sqrt).then_inc(s["std_ready"], 1)
                act.wait_ge(s["xt_done"], w + 1)
                act.wait_ge(s["projected"], w)
                act.wait_ge(s["h0_stored"], 16 * w)
                act.activation(Y[0:C, :], psT[0:C, 0:WIN], ACT.Copy).then_inc(s["y_ready"], 1)
                copy_projection(0, w)
            general(0)
            finish(0)
            with act.Fori(0, NW) as w:
                act.wait_ge(s["y_ready"], w + NW)
                act.activation(lin[0:C, :], acc[0:C, bass.ds(w * WIN, WIN)], ACT.Identity, bias=stat[0:C, 6:7], scale=stat[0:C, 5:6]).then_inc(s["lin_ready"], 1)
                copy_projection(1, w)
            general(1)
            finish(1)
            with act.Fori(0, NW) as w:
                act.wait_ge(s["v_ready"], w)
                act.activation(lin[0:C, :], acc[0:C, bass.ds(w * WIN, WIN)], ACT.Identity, bias=stat[0:C, 6:7], scale=stat[0:C, 5:6]).then_inc(s["lin_ready"], 1)

        @block.tensor
        def _(pe):
            pe.wait_ge(s["consts_made"], 1)
            pe.wait_ge(s["weights_in"], 16 * 11)
            for l in range(2):
                pe.transpose(psT[0:C, l * C:(l + 1) * C], wraw[0:C, l, :], ident[0:C, 0:C])
                pe.matmul(psT[0:C, 2 * C + 2 * l:2 * C + 2 * l + 2], wraw[0:C, l, :], avec[0:C, 2 * l:2 * l + 2], start=True, stop=True).then_inc(s["wt_psum"], 1)
            pe.wait_ge(s["wt_copied"], 4)

            def project(l, w):
                turn = l * NW + w
                pe.wait_ge(s["y_ready"], turn + 1)
                pe.wait_ge(s["h_copied"], 2 * turn)
                pe.matmul(psH[0:C + 1, 0:WIN], wext[0:C + 1, l, 0:C + 1], Y[0:C + 1, :], start=True, stop=True)
                for b in range(BPW):
                    last = pe.matmul(psTab[0:BLOCK, b * EXT:(b + 1) * EXT], Y[0:C + 1, b * BLOCK:(b + 1) * BLOCK], wext[0:C + 1, l, :], start=True, stop=True)
                last.then_inc(s["projected"], 1)

            def general(l):
                with pe.Fori(0, TILES) as t:
                    pe.wait_ge(g[l]["e_diag"], t + 1)
                    pe.matmul(psE[:, 0:P], ones[:, :], g_diag[:, :], start=True, stop=True).then_inc(g[l]["e_row"], 1)
                    pe.wait_ge(g[l]["e_weighted"], t + 1)
                    pe.matmul(psU[:, 0:C + 1], g_eq[:, :], g_w[:, 0:C + 1], start=True, stop=True).then_inc(g[l]["e_sum"], 1)
                with pe.Fori(0, NW) as w:
                    turn = w
                    pe.wait_ge(g[l]["gb_ready"], turn + 1)
                    pe.wait_ge(g[l]["gb_copied"], turn)
                    for b in range(BPW):
                        last = pe.transpose(psT[0:STATE, b * BLOCK:(b + 1) * BLOCK], g_init[0:BLOCK, b, :], ident[0:BLOCK, 0:BLOCK])
                    last.then_inc(g[l]["gb_turned"], 1)

            def finish(l):
                pe.wait_ge(g[l]["gb_copied"], NW)
                with pe.Fori(0, NW) as w:
                    turn = w + l * NW
                    win = bass.ds(w * WIN, WIN)
                    pe.wait_ge(s["self_weight"], turn)
                    pe.matmul(psD[0:C + 1, 0:WIN], sel_delta[0:C + 2, 0:C + 1], acc[0:C + 2, win], start=True, stop=True).then_inc(s["delta_spread"], 1)
                    pe.wait_ge(s["total_ready"], turn + 1)
                    pe.wait_ge(s["norm_ready"], turn)
                    pe.matmul(psZ[0:C, 0:WIN], sel_z[0:C + 1, 0:C], acc[0:C + 1, win], start=True, stop=True).then_inc(s["z_spread"], 1)

            with pe.Fori(0, NW) as w:
                pe.wait_ge(s["xn_ready"], w + 1)
                pe.wait_ge(s["y_ready"], w)
                for b in range(BPW):
                    last = pe.transpose(psT[0:C, b * BLOCK:(b + 1) * BLOCK], xn[0:BLOCK, b, :], ident[0:BLOCK, 0:BLOCK])
                last.then_inc(s["xt_done"], 1)
                project(0, w)
            general(0)
            finish(0)
            with pe.Fori(0, NW) as w:
                project(1, w)
            general(1)
            finish(1)
            with pe.Fori(0, NW) as w:
                pe.wait_ge(s["v_ready"], w + 1)
                pe.wait_ge(s["out_ready"], w)
                for b in range(BPW):
                    last = pe.transpose(psTab[0:BLOCK, b * C:(b + 1) * C], Y[0:C, b * BLOCK:(b + 1) * BLOCK], ident[0:C, 0:C])
                last.then_inc(s["v_back"], 1)

        @block.vector
        def _(dve):
            own = Chain(dve, s["own_vector"])
            link = own.link

            def general(l):
                with dve.Fori(0, NW) as w:
                    turn = w
                    own.enter(w, 2)
                    dve.wait_ge(g[l]["gi_in"], 32 * turn + 32)
                    link(dve.tensor_tensor(xs[0:BLOCK, 0, :], g_alph[0:BLOCK, :, 0], g_alph[0:BLOCK, :, 1], ALU.add))
                    link(dve.tensor_copy(g_init[0:BLOCK, :, C + 2:C + 3], g_alph[0:BLOCK, :, 1:2]))
                    dve.scalar_tensor_tensor(out=g_init[0:BLOCK, :, C + 1], in0=xs[0:BLOCK, 0, :], scalar=SLOPE_ATT, in1=xs[0:BLOCK, 0, :],
                                             op0=ALU.mult, op1=ALU.max).then_inc(g[l]["gi_ready"], 1)
                own.leave(NW)
                with dve.Fori(0, TILES) as t:
                    own.enter(t, 12)
                    dve.wait_ge(g[l]["e_dst"], 16 * t + 16)
                    dve.wait_ge(g[l]["e_dstrow"], 16 * t + 16)
                    dve.wait_ge(g[l]["e_scattered"], 16 * t)
                    link(dve.tensor_copy(g_c[:, 0:1], g_dst[:, :]))
                    link(dve.tensor_copy(g_tmp[:, :], g_dstrow[:, :]))
                    link(dve.tensor_scalar(g_eq[:, :], g_tmp[:, :], g_c[:, 0:1], None, ALU.is_equal))
                    link(dve.tensor_tensor(g_tmp[:, :], g_eq[:, :], lower[:, :], ALU.mult))
                    link(dve.tensor_reduce(g_c[:, 1:2], g_tmp[:, :], AX, ALU.add))
                    dve.scalar_tensor_tensor(out=g_sidx[:, :], in0=g_c[:, 1:2], scalar=1e6, in1=g_c[:, 0:1], op0=ALU.mult, op1=ALU.add)
                    dve.wait_ge(g[l]["e_rows"], 16 * t + 16)
                    dve.wait_ge(g[l]["e_old"], 16 * t + 16)
                    link(dve.tensor_tensor(g_c[:, 6:7], g_rows[:, C + 1:C + 2], g_old[:, C + 2:C + 3], ALU.add))
                    link(dve.scalar_tensor_tensor(out=g_c[:, 1:2], in0=g_c[:, 6:7], scalar=SLOPE_ATT, in1=g_c[:, 6:7], op0=ALU.mult, op1=ALU.max))
                    dve.tensor_scalar(g_diag[:, :], ident[:, :], g_c[:, 1:2], None, ALU.mult).then_inc(g[l]["e_diag"], 1)
                    link(dve.tensor_scalar(g_tmp[:, :], g_eq[:, :], BIG, -BIG, ALU.mult, ALU.add))
                    dve.wait_ge(g[l]["e_row"], t + 1)
                    link(dve.tensor_tensor(g_tmp[:, :], g_tmp[:, :], psE[:, 0:P], ALU.add))
                    link(dve.tensor_reduce(g_c[:, 6:7], g_tmp[:, :], AX, ALU.max))
                    link(dve.tensor_tensor(g_new[:, C + 1:C + 2], g_c[:, 6:7], g_old[:, C + 1:C + 2], ALU.max))
                    dve.tensor_tensor(g_c[:, 2:3], g_old[:, C + 1:C + 2], g_new[:, C + 1:C + 2], ALU.subtract)
                    link(dve.tensor_tensor(g_c[:, 3:4], g_c[:, 1:2], g_new[:, C + 1:C + 2], ALU.subtract))
                    dve.tensor_copy(g_new[:, C + 2:C + 3], g_old[:, C + 2:C + 3]).then_inc(g[l]["e_wt"], 1)
                    dve.wait_ge(g[l]["e_exp"], t + 1)
                    dve.tensor_scalar(g_w[:, 0:C + 1], g_rows[:, 0:C + 1], g_c[:, 5:6], None, ALU.mult).then_inc(g[l]["e_weighted"], 1)
                    dve.wait_ge(g[l]["e_sum"], t + 1)
                    dve.scalar_tensor_tensor(out=g_new[:, 0:C + 1], in0=g_old[:, 0:C + 1], scalar=g_c[:, 4:5], in1=psU[:, 0:C + 1],
                                             op0=ALU.mult, op1=ALU.add).then_inc(g[l]["e_new"], 1)
                own.leave(TILES)
                with dve.Fori(0, NW) as w:
                    dve.wait_ge(g[l]["gb_in"], 16 * w + 16)
                    dve.memset(g_init[0:BLOCK, :, C + 1:C + 2], 1e4).then_inc(g[l]["gb_ready"], 1)

            def finish(l):
                with dve.Fori(0, NW) as w:
                    turn = w + l * NW
                    win = bass.ds(w * WIN, WIN)
                    own.enter(w, 2)
                    dve.wait_ge(s["self_weight"], turn + 1)
                    link(dve.tensor_tensor(lin[0:C + 1, :], lin[0:C + 1, :], ht[0:C + 1, win], ALU.mult))
                    dve.tensor_tensor(acc[0:C + 1, win], acc[0:C + 1, win], lin[0:C + 1, :], ALU.add).then_inc(s["total_ready"], 1)
                    dve.wait_ge(s["z_spread"], turn + 1)
                    link(dve.reciprocal(res[0:C, :], psZ[0:C, 0:WIN]))
                    dve.tensor_tensor(acc[0:C, win], acc[0:C, win], res[0:C, :], ALU.mult).then_inc(s["norm_ready"], 1)
                own.leave(NW)
                dve.wait_ge(s["sum_ready"], l + 1)
                link(dve.tensor_scalar(stat[0:C, 7:8], stat[0:C, 0:1], -1.0 / N, None, ALU.mult))
                dve.tensor_tensor(stat[0:C, 1:2], stat[0:C, 7:8], gn[0:C, 4:5], ALU.mult).then_inc(s["shift_ready"], 1)
                dve.wait_ge(s["square_ready"], l + 1)
                dve.tensor_scalar(stat[0:C, 3:4], stat[0:C, 2:3], 1.0 / N, EPS, ALU.mult, ALU.add).then_inc(s["var_ready"], 1)
                dve.wait_ge(s["gn_std"], l + 1)
                link(dve.reciprocal(stat[0:C, 7:8], stat[0:C, 4:5]))
                link(dve.tensor_tensor(stat[0:C, 5:6], stat[0:C, 7:8], gn[0:C, 2:3], ALU.mult))
                link(dve.tensor_tensor(stat[0:C, 7:8], stat[0:C, 5:6], stat[0:C, 1:2], ALU.mult))
                dve.tensor_tensor(stat[0:C, 6:7], stat[0:C, 7:8], gn[0:C, 3:4], ALU.add).then_inc(s["gn_ready"], 1)

            with dve.Fori(0, NW) as w:
                own.enter(w, 6)
                dve.wait_ge(s["x_in"], 16 * w + 16)
                link(dve.tensor_reduce(xs[0:BLOCK, 0, :], xin[0:BLOCK, :, :], AX, ALU.add))
                link(dve.tensor_scalar(xs[0:BLOCK, 3, :], xs[0:BLOCK, 0, :], 1.0 / C, None, ALU.mult))
                link(dve.tensor_tensor(xc[0:BLOCK, :, :], xin[0:BLOCK, :, :], xs[0:BLOCK, 3, :].unsqueeze(2).to_broadcast([BLOCK, BPW, C]), ALU.subtract))
                dve.wait_ge(s["xt_done"], w)
                link(dve.tensor_tensor(xn[0:BLOCK, :, :], xc[0:BLOCK, :, :], xc[0:BLOCK, :, :], ALU.mult))
                link(dve.tensor_reduce(xs[0:BLOCK, 0, :], xn[0:BLOCK, :, :], AX, ALU.add))
                dve.tensor_scalar(xs[0:BLOCK, 1, :], xs[0:BLOCK, 0, :], 1.0 / C, EPS, ALU.mult, ALU.add).then_inc(s["var_ready"], 1)
                dve.wait_ge(s["std_ready"], w + 1)
                link(dve.reciprocal(xs[0:BLOCK, 3, :], xs[0:BLOCK, 2, :]))
                dve.scalar_tensor_tensor(out=xn[0:BLOCK, :, :], in0=xc[0:BLOCK, :, :], scalar=0.0,
                                         in1=xs[0:BLOCK, 3, :].unsqueeze(2).to_broadcast([BLOCK, BPW, C]), op0=ALU.max, op1=ALU.mult).then_inc(s["xn_ready"], 1)
            own.leave(NW)
            general(0)
            finish(0)
            with dve.Fori(0, NW) as w:
                dve.wait_ge(s["lin_ready"], w + 1)
                dve.wait_ge(s["projected"], w + NW)
                dve.scalar_tensor_tensor(out=Y[0:C, :], in0=lin[0:C, :], scalar=SLOPE_ACT, in1=lin[0:C, :], op0=ALU.mult, op1=ALU.max).then_inc(s["y_ready"], 1)
            general(1)
            finish(1)
            with dve.Fori(0, NW) as w:
                own.enter(w, 1)
                dve.wait_ge(s["lin_ready"], w + NW + 1)
                dve.wait_ge(s["res_in"], 16 * w + 16)
                link(dve.tensor_tensor(res[0:C, :], lin[0:C, :], res[0:C, :], ALU.add))
                dve.scalar_tensor_tensor(out=Y[0:C, :], in0=res[0:C, :], scalar=SLOPE_ACT, in1=res[0:C, :], op0=ALU.mult, op1=ALU.max).then_inc(s["v_ready"], 1)
                dve.wait_ge(s["v_back"], w + 1)
                dve.wait_ge(s["x_in"], 16 * (w + NW) + 16)
                dve.wait_ge(s["out_written"], 16 * w)
                dve.tensor_tensor(xn[0:BLOCK, :, :], psTab[0:BLOCK, 0:BPW * C].rearrange("p (b c) -> p b c", b=BPW), xin[0:BLOCK, :, :], ALU.add).then_inc(s["out_ready"], 1)
            own.leave(NW)


_INS = ["x", "src", "dst", "L0_gnn_W1", "L0_gnn_att_src1", "L0_gnn_att_dst1", "L0_gnn_b1", "L0_gnn_W2", "L0_gnn_att_src2",
        "L0_gnn_att_dst2", "L0_gnn_b2", "L0_gnn_gn_weight", "L0_gnn_gn_bias", "L0_gnn_gn_mean_scale"]


def kernel(**inputs):
    import numpy as _np
    import concourse.bacc as _bacc
    from concourse import mybir as _mybir
    from concourse.bass_utils import run_bass_kernel_spmd as _run

    nc = _bacc.Bacc("TRN2", target_bir_lowering=False, num_devices=1)
    arrays, args = {}, []
    for name in _INS:
        a = _np.ascontiguousarray(inputs[name])
        arrays[f"in_{name}_dram"] = a
        args.append(nc.dram_tensor(f"in_{name}_dram", a.shape, _mybir.dt.from_np(a.dtype), kind="ExternalInput").ap())
    args.append(nc.dram_tensor("out_0_dram", inputs["x"].shape, _mybir.dt.float32, kind="ExternalOutput").ap())
    gat_kernel(nc, *args)
    r = _run(nc, [arrays], core_ids=[0])
    return r.results[0]["out_0_dram"]
```

```python
from contextlib import ExitStack

import concourse.bass as bass
from concourse import mybir

P = 128
C = 96
BLOCK = 125
BPW = 4
WIN = BLOCK * BPW
TAB = C + 2
EXT = C + 3
STATE = C + 3
SLOPE_ATT = 0.2
SLOPE_ACT = 0.01
EPS = 1e-5
BIG = 1e30
CT = 25
GT = 5
GROUPS = CT // GT
W = 64
RING = 5
TRIO = [0, 1, 2, 0, 1]
CE = CT * P

ALU = mybir.AluOpType
ACT = mybir.ActivationFunctionType
F32 = mybir.dt.float32
I32 = mybir.dt.int32
AX = mybir.AxisListType.X


class Chain:

    def __init__(self, eng, sem):
        self.eng, self.sem, self.n, self.turn = eng, sem, 0, 0

    def link(self, ins):
        ins.then_inc(self.sem, 1)
        self.n += 1
        self.eng.wait_ge(self.sem, self.turn + self.n)

    def enter(self, i, per):
        self.turn, self.first, self.per = i * per, self.n, per

    def leave(self, count):
        assert self.n - self.first == self.per, (self.n - self.first, self.per)
        self.turn, self.n = 0, self.first + self.per * count


def gat_kernel(nc, x, src, dst, W1, as1, ad1, b1, W2, as2, ad2, b2, gn_w, gn_b, gn_ms, out):
    N = x.shape[0]
    E = src.shape[0]
    NW = N // WIN
    TILES = E // P
    NCH = TILES // CT
    NG = NCH * GROUPS
    assert TILES % CT == 0 and NCH <= P and (NCH <= 2 * RING or NCH % RING == 0)
    assert N % WIN == 0 and E % P == 0 and x.shape[1] == C

    with ExitStack() as ctx:
        def sb(name, shape, dt=F32):
            return ctx.enter_context(nc.sbuf_tensor(name, shape, dt))

        def ps(name, shape):
            return ctx.enter_context(nc.psum_tensor(name, shape, F32))

        def sem(name):
            return ctx.enter_context(nc.semaphore(name))

        def dram(name, shape, dt=F32):
            return nc.dram_tensor(name, shape, dt, kind="Internal").ap()

        table = dram("table", [N, TAB])
        alphas = dram("alphas", [N + W, 2])
        dst_pad = dram("dst_pad", [E + 2], I32)
        ht_d = dram("ht_d", [C + 1, N])
        state = dram("state", [N, STATE])
        h0t = dram("h0t", [C, N])

        acc = sb("acc", [P, N + W])
        big = sb("big", [P, max(N, RING * CT * TAB, 2 * CE + 1)])
        rows = big[:, 0:RING * CT * TAB].rearrange("p (r t c) -> p r t c", r=RING, t=CT)
        hs = sb("hs", [P, WIN])
        zeros = sb("zeros", [P, WIN])
        iota = sb("iota", [P, W])
        iota_i = sb("iota_i", [P, W], I32)
        minus = sb("minus", [P, 2], I32)
        zero_win = sb("zero_win", [P, 2])
        first_i = sb("first_i", [P, NG], I32)
        last_i = sb("last_i", [P, NG], I32)
        first_f = sb("first_f", [P, NG])
        last_f = sb("last_f", [P, NG])
        first_all = sb("first_all", [P, NG])
        viol = sb("viol", [P, 4])
        flag = sb("flag", [P, 1], I32)
        t_int = sb("t_int", [P, 3, 4, P], I32)
        t_flt = sb("t_flt", [P, 3, 3, P])
        t_pen = sb("t_pen", [P, 3, P])
        t_v = sb("t_v", [P, P])
        t_m = sb("t_m", [P, P])
        row_v = sb("row_v", [P, CE])
        row_pen = sb("row_pen", [P, CE + 1])
        carry = sb("carry", [P, 1])
        fr = sb("fr", [P, 4])
        c_idx = sb("c_idx", [P, RING, CT], I32)
        c_dl = sb("c_dl", [P, RING, 2, CT])
        c_own = sb("c_own", [P, RING, 2, CT])
        c_v = sb("c_v", [P, CT])
        c_q = sb("c_q", [P, 3, CT])
        c_s = sb("c_s", [P, 3, CT])
        c_w = sb("c_w", [P, CT])
        a_win = sb("a_win", [P, 3, GROUPS, W, 2])
        onehot = sb("onehot", [P, 3, CT, W])
        prod = sb("prod", [P, CT, W])
        ident = sb("ident", [P, P])
        ones = sb("ones", [P, P])
        lower = sb("lower", [P, P])
        sel_delta = sb("sel_delta", [P, P])
        sel_z = sb("sel_z", [P, P])
        wraw = sb("wraw", [P, 2, C])
        avec = sb("avec", [P, 4])
        wext = sb("wext", [P, 2, EXT])
        gn = sb("gn", [P, 5])
        stat = sb("stat", [P, 8])
        xin = sb("xin", [P, BPW, C])
        xc = sb("xc", [P, BPW, C])
        xn = sb("xn", [P, BPW, C])
        xs = sb("xs", [P, 4, BPW])
        Y = sb("Y", [P, WIN])
        tabs = sb("tabs", [P, BPW, EXT])
        lin = sb("lin", [P, WIN])
        res = sb("res", [P, WIN])
        flat = prod[:, :, :].rearrange("p t w -> p (t w)")
        taken = [0]

        def part(width):
            taken[0] += width
            return flat[:, taken[0] - width:taken[0]]

        g_rows = part(TAB)
        g_old = part(STATE)
        g_new = part(STATE)
        g_eq = part(P)
        g_tmp = part(P)
        g_diag = part(P)
        g_w = part(TAB)
        g_c = part(8)
        g_init = part(BPW * STATE).rearrange("p (b c) -> p b c", b=BPW)
        g_alph = part(BPW * 2).rearrange("p (b c) -> p b c", b=BPW)
        assert taken[0] <= CT * W
        g_src = sb("g_src", [P, 1], I32)
        g_dst = sb("g_dst", [P, 1], I32)
        g_dstrow = sb("g_dstrow", [P, P], I32)
        g_sidx = sb("g_sidx", [P, 1], I32)

        psT = ps("psT", [P, 512])
        psH = ps("psH", [P, 512])
        psTab = ps("psTab", [P, 512])
        psD = ps("psD", [P, 512])
        psZ = ps("psZ", [P, 512])
        psE = ps("psE", [P, 512])
        psU = ps("psU", [P, 512])
        psW = [psD, psZ, psE]

        names = """weights_in consts_made own_vector own_scalar own_pool pool_passed sp_passed pe_passed
        pad_written firsts_in first_row first_spread check_in checked flag_psum flag_ready h_in
        prep_in prep_made turned idx_ready dl_ready awin_in expanded v_col v_turned vt_ready vrow_in penrow_in scanned mrow_back m_turned
        scored factor_ready factor_spread scaled summed added ext_made wt_psum wt_copied x_in xn_ready xt_done var_ready
        std_ready y_ready projected h_copied table_written h0_stored
        delta_spread self_weight total_ready z_spread norm_ready sum_ready shift_ready square_ready gn_std
        gn_ready lin_ready res_in v_ready v_back out_ready out_written
"""
        s = {k: sem(k) for k in names.split()}
        edge_names = """gi_in gi_ready gi_written e_src e_dst e_dstrow e_rows e_old e_new e_scattered e_diag e_row e_wt e_exp e_weighted e_sum
        gb_in gb_ready gb_turned gb_copied"""
        own_sems = {(e, path, l): sem(f"own_{e}_{path}_{l}") for e in ("vector", "scalar") for path in ("fast", "general") for l in range(2)}
        gathered = [sem(f"gathered_{r}") for r in range(RING)]
        g = [{k: sem(f"{k}_{l}") for k in edge_names.split()} for l in range(2)]

        def since(eng, name, value):
            if not isinstance(value, int) or value > 0:
                eng.wait_ge(name if not isinstance(name, str) else s[name], value)

        def exists(c):
            return not isinstance(c, int) or 0 <= c < NCH

        def over_chunks(eng, turn, chain=None, per_turn=0):
            if NCH <= 2 * RING:
                for c in range(NCH):
                    turn(c, c % RING)
                return
            for c in range(RING):
                turn(c, c)
            with eng.Fori(1, NCH // RING - 1) as i:
                if chain:
                    chain.enter(i - 1, per_turn * RING)
                for r in range(RING):
                    turn(i * RING + r, r)
            if chain:
                chain.leave(NCH // RING - 2)
            for c in range(NCH - RING, NCH):
                turn(c, c % RING)

        def by_order(eng, regflag, fast, general, l):
            with eng.If(regflag < 1):
                fast(l)
            with eng.Else():
                general(l)

        def x_window(w):
            return x[bass.ds(w * WIN, WIN), :].rearrange("(b p) c -> p b c", p=BLOCK)

        block = ctx.enter_context(nc.Block())

        @block.sync
        def _(sp):
            for i, (dst_ap, src_ap) in enumerate((
                    (wraw[0:C, 0, :], W1), (wraw[0:C, 1, :], W2),
                    (avec[0:C, 0:1], as1.rearrange("(c a) -> c a", a=1)), (avec[0:C, 1:2], ad1.rearrange("(c a) -> c a", a=1)),
                    (avec[0:C, 2:3], as2.rearrange("(c a) -> c a", a=1)), (avec[0:C, 3:4], ad2.rearrange("(c a) -> c a", a=1)),
                    (gn[0:C, 0:1], b1.rearrange("(c a) -> c a", a=1)), (gn[0:C, 1:2], b2.rearrange("(c a) -> c a", a=1)),
                    (gn[0:C, 2:3], gn_w.rearrange("(c a) -> c a", a=1)), (gn[0:C, 3:4], gn_b.rearrange("(c a) -> c a", a=1)),
                    (gn[0:C, 4:5], gn_ms.rearrange("(c a) -> c a", a=1)))):
                sp.dma_start(dst_ap, src_ap).then_inc(s["weights_in"], 16)

            sp.wait_ge(s["consts_made"], 1)
            sp.dma_start(dst_pad[1:E + 1].rearrange("(p a) -> p a", p=P), dst.rearrange("(p a) -> p a", p=P)).then_inc(s["pad_written"], 16)
            sp.dma_start(dst_pad[0:1].rearrange("(p a) -> p a", p=1), minus[0:1, 0:1]).then_inc(s["pad_written"], 16)
            sp.dma_start(dst_pad[E + 1:E + 2].rearrange("(p a) -> p a", p=1), minus[0:1, 1:2]).then_inc(s["pad_written"], 16)
            sp.dma_start(alphas[N:N + W, :], zero_win[0:W, :]).then_inc(s["pad_written"], 16)
            by_group = dst.rearrange("(g a) -> a g", a=GT * P)
            sp.dma_start(first_i[0:1, :], by_group[0:1, :], allow_slow_non_contiguous=True).then_inc(s["firsts_in"], 16)
            sp.dma_start(last_i[0:1, :], by_group[GT * P - 1:GT * P, :], allow_slow_non_contiguous=True).then_inc(s["firsts_in"], 16)
            sp.wait_ge(s["pad_written"], 64)
            sp.dma_start(big[0:NCH, 0:CE].bitcast(I32), dst_pad[0:E].rearrange("(c e) -> c e", e=CE)).then_inc(s["check_in"], 16)
            sp.dma_start(big[0:NCH, CE:2 * CE].bitcast(I32), dst_pad[1:E + 1].rearrange("(c e) -> c e", e=CE)).then_inc(s["check_in"], 16)

            def fast(l):
                def load_indices(c, r):
                    if not exists(c):
                        return
                    q = l * NCH + c
                    since(sp, "prep_made", q)
                    sp.sem_inc(s["sp_passed"], 1)
                    for k, (ap, shift) in enumerate(((src, 0), (dst_pad, 1), (dst_pad, 0), (dst_pad, 2))):
                        sp.dma_start(t_int[0:CT, TRIO[r], k, :], ap[bass.ds(c * CE + shift, CE)].rearrange("(t p) -> t p", p=P)).then_inc(s["prep_in"], 16)

                def load_windows(c, r):
                    if not exists(c):
                        return
                    q = l * NCH + c
                    since(sp, "expanded", q)
                    sp.sem_inc(s["sp_passed"], 1)
                    for k in range(GROUPS):
                        first = sp.value_load(first_i[0:1, bass.ds(c * GROUPS + k, 1)], min_val=0, max_val=N - 1)
                        sp.dma_start(a_win[:, TRIO[r], k, :, :].rearrange("p w k -> p (w k)"),
                                     alphas[bass.ds(first, W), :].rearrange("(a w) k -> a (w k)", a=1).to_broadcast([P, 2 * W])).then_inc(s["awin_in"], 16)

                def penalties(c, r):
                    if not exists(c):
                        return
                    q = l * NCH + c
                    since(sp, "scanned", q)
                    sp.sem_inc(s["sp_passed"], 1)
                    sp.wait_ge(s["prep_made"], q + 1)
                    sp.sem_inc(s["sp_passed"], 1)
                    sp.dma_start(row_pen[0:1, 0:CE], t_pen[0:CT, TRIO[r], :]).then_inc(s["penrow_in"], 16)

                def turn(c, r):
                    q = l * NCH + c
                    sp.wait_ge(s["vt_ready"], q + 1)
                    sp.sem_inc(s["sp_passed"], 1)
                    sp.dma_start(row_v[0:1, :], t_v[0:CT, :]).then_inc(s["vrow_in"], 16)
                    load_indices(c + 3, (r + 3) % RING)
                    since(sp, "m_turned", q)
                    sp.sem_inc(s["sp_passed"], 1)
                    sp.wait_ge(s["scanned"], q + 1)
                    sp.sem_inc(s["sp_passed"], 1)
                    sp.dma_start(t_m[0:CT, :], row_v[0:1, :]).then_inc(s["mrow_back"], 16)
                    penalties(c + 1, (r + 1) % RING)
                    load_windows(c + 2, (r + 2) % RING)

                sp.wait_ge(s["table_written"], 48 * NW * (l + 1))
                for c in range(3):
                    load_indices(c, c)
                penalties(0, 0)
                for c in range(2):
                    load_windows(c, c)
                over_chunks(sp, turn)

            def load_projection(l):
                with sp.Fori(0, NW) as w:
                    turn = w + l * NW
                    sp.wait_ge(s["total_ready"], turn)
                    sp.sem_inc(s["sp_passed"], 1)
                    sp.dma_start(hs[0:C + 1, :], ht_d[:, bass.ds(w * WIN, WIN)]).then_inc(s["h_in"], 16)

            def write_table(l, w):
                turn = l * NW + w
                sp.wait_ge(s["h_copied"], 2 * turn + 2)
                sp.dma_start(table[bass.ds(w * WIN, WIN), :].rearrange("(b p) c -> p b c", p=BLOCK),
                             tabs[0:BLOCK, :, 0:TAB]).then_inc(s["table_written"], 16)
                sp.dma_start(alphas[bass.ds(w * WIN, WIN), :].rearrange("(b p) c -> p b c", p=BLOCK),
                             tabs[0:BLOCK, :, C + 1:EXT]).then_inc(s["table_written"], 16)
                sp.dma_start(ht_d[:, bass.ds(w * WIN, WIN)], hs[0:C + 1, :]).then_inc(s["table_written"], 16)

            def general(l):
                sp.wait_ge(s["table_written"], 48 * NW * (l + 1))
                with sp.Fori(0, NW) as w:
                    turn = w
                    sp.wait_ge(g[l]["gi_written"], 16 * turn)
                    sp.dma_start(g_init[0:BLOCK, :, 0:TAB], table[bass.ds(w * WIN, WIN), :].rearrange("(b p) c -> p b c", p=BLOCK)).then_inc(g[l]["gi_in"], 16)
                    sp.dma_start(g_alph[0:BLOCK, :, :], alphas[bass.ds(w * WIN, WIN), :].rearrange("(b p) c -> p b c", p=BLOCK)).then_inc(g[l]["gi_in"], 16)
                    sp.wait_ge(g[l]["gi_ready"], turn + 1)
                    sp.dma_start(state[bass.ds(w * WIN, WIN), :].rearrange("(b p) c -> p b c", p=BLOCK), g_init[0:BLOCK, :, :]).then_inc(g[l]["gi_written"], 16)
                with sp.Fori(0, TILES) as t:
                    sp.wait_ge(g[l]["e_scattered"], 16 * t)
                    sp.dma_start(g_src[:, :], src[bass.ds(t * P, P)].rearrange("(p a) -> p a", a=1)).then_inc(g[l]["e_src"], 16)
                    sp.dma_start(g_dst[:, :], dst[bass.ds(t * P, P)].rearrange("(p a) -> p a", a=1)).then_inc(g[l]["e_dst"], 16)
                    sp.dma_start(g_dstrow[:, :], dst[bass.ds(t * P, P)].rearrange("(a p) -> a p", a=1).to_broadcast([P, P])).then_inc(g[l]["e_dstrow"], 16)
                sp.wait_ge(g[l]["e_scattered"], 16 * TILES)
                with sp.Fori(0, NW) as w:
                    turn = w
                    sp.wait_ge(g[l]["gb_turned"], turn)
                    sp.dma_start(g_init[0:BLOCK, :, :], state[bass.ds(w * WIN, WIN), :].rearrange("(b p) c -> p b c", p=BLOCK)).then_inc(g[l]["gb_in"], 16)

            with sp.Fori(0, NW) as w:
                sp.wait_ge(s["xn_ready"], w)
                sp.dma_start(xin[0:BLOCK, :, :], x_window(w)).then_inc(s["x_in"], 16)
                sp.wait_ge(s["y_ready"], w + 1)
                sp.sem_inc(s["sp_passed"], 1)
                sp.dma_start(h0t[:, bass.ds(w * WIN, WIN)], Y[0:C, :]).then_inc(s["h0_stored"], 16)
                write_table(0, w)
            sp.wait_ge(s["flag_ready"], 1)
            unordered = sp.value_load(flag[0:1, 0:1], min_val=0, max_val=1)
            by_order(sp, unordered, fast, general, 0)
            load_projection(0)
            with sp.Fori(0, NW) as w:
                write_table(1, w)
            by_order(sp, unordered, fast, general, 1)
            load_projection(1)
            sp.wait_ge(s["gn_ready"], 2)
            with sp.Fori(0, NW) as w:
                sp.wait_ge(s["v_ready"], w)
                sp.dma_start(res[0:C, :], h0t[:, bass.ds(w * WIN, WIN)]).then_inc(s["res_in"], 16)
                sp.wait_ge(s["out_ready"], w)
                sp.dma_start(xin[0:BLOCK, :, :], x_window(w)).then_inc(s["x_in"], 16)
                sp.wait_ge(s["out_ready"], w + 1)
                sp.dma_start(out[bass.ds(w * WIN, WIN), :].rearrange("(b p) c -> p b c", p=BLOCK), xn[0:BLOCK, :, :]).then_inc(s["out_written"], 16)
            sp.wait_ge(s["out_written"], 16 * NW)

        @block.gpsimd
        def _(pool):
            made = Chain(pool, s["own_pool"])
            made.link(pool.memset(ident[:, :], 0.0))
            made.link(pool.memset(ones[:, :], 1.0))
            made.link(pool.memset(sel_delta[:, :], 0.0))
            made.link(pool.memset(sel_z[:, :], 0.0))
            made.link(pool.affine_select(out=ident[:, :], in_=ident[:, :], compare_op=ALU.not_equal, fill=1.0, base=0,
                                         pattern=[[-1, P]], channel_multiplier=1))
            made.link(pool.affine_select(out=lower[:, :], in_=ones[:, :], compare_op=ALU.is_gt, fill=0.0, base=0,
                                         pattern=[[-1, P]], channel_multiplier=1))
            made.link(pool.affine_select(out=sel_delta[:, :], in_=sel_delta[:, :], compare_op=ALU.not_equal, fill=1.0,
                                         base=-(C + 1), pattern=[[0, P]], channel_multiplier=1))
            made.link(pool.affine_select(out=sel_z[:, :], in_=sel_z[:, :], compare_op=ALU.not_equal, fill=1.0,
                                         base=-C, pattern=[[0, P]], channel_multiplier=1))
            made.link(pool.memset(wext[:, :, :], 0.0))
            made.link(pool.memset(wext[C:C + 1, :, C:C + 1], 1.0))
            made.link(pool.memset(minus[:, :], -1))
            made.link(pool.memset(zero_win[:, :], 0.0))
            made.link(pool.iota(iota_i[:, :], pattern=[[1, W]], base=0, channel_multiplier=0))
            made.link(pool.tensor_copy(iota[:, :], iota_i[:, :]))
            made.link(pool.memset(zeros[:, :], 0.0))
            made.link(pool.memset(row_pen[0:1, CE:CE + 1], -BIG))
            made.link(pool.memset(Y[C:C + 1, :], 1.0))
            pool.memset(acc[:, :], 0.0).then_inc(s["consts_made"], 1)

            def fast(l):
                def turn(c, r):
                    q = l * NCH + c
                    pool.wait_ge(s["idx_ready"], q + 1)
                    since(pool, "summed", q + 1 - RING)
                    pool.sem_inc(s["pool_passed"], 1)
                    for t in range(CT):
                        pool.indirect_dma_start(rows[:, r, t, :], None, table,
                                                bass.IndirectOffsetOnAxis(ap=c_idx[:, r, t:t + 1], axis=0)).then_inc(gathered[r], 16)

                over_chunks(pool, turn)
                for r in range(min(RING, NCH)):
                    pool.wait_ge(gathered[r], 16 * CT * len(range(r, NCH, RING)) * (l + 1))

            last_node = pool.to_reg(N - 1)

            def general(l):
                pool.wait_ge(g[l]["gi_written"], 16 * NW)
                with pool.Fori(0, TILES) as t:
                    pool.wait_ge(g[l]["e_src"], 16 * t + 16)
                    pool.wait_ge(g[l]["e_dst"], 16 * t + 16)
                    pool.wait_ge(g[l]["e_scattered"], 16 * t)
                    pool.sem_inc(s["pool_passed"], 1)
                    pool.indirect_dma_start(g_rows[:, :], None, table, bass.IndirectOffsetOnAxis(ap=g_src[:, 0:1], axis=0)).then_inc(g[l]["e_rows"], 16)
                    pool.indirect_dma_start(g_old[:, :], None, state, bass.IndirectOffsetOnAxis(ap=g_dst[:, 0:1], axis=0)).then_inc(g[l]["e_old"], 16)
                    pool.wait_ge(g[l]["e_new"], t + 1)
                    pool.sem_inc(s["pool_passed"], 1)
                    pool.indirect_dma_start(state, bass.IndirectOffsetOnAxis(ap=g_sidx[:, 0:1], axis=0), g_new[:, :], None,
                                            bounds_check=last_node, oob_is_err=False).then_inc(g[l]["e_scattered"], 16)
                pool.wait_ge(g[l]["e_scattered"], 16 * TILES)

            pool.wait_ge(s["flag_ready"], 1)
            unordered = pool.value_load(flag[0:1, 0:1], min_val=0, max_val=1)
            for l in range(2):
                pool.wait_ge(s["table_written"], 48 * NW * (l + 1))
                by_order(pool, unordered, fast, general, l)

        @block.scalar
        def _(act):
            def copy_projection(l, w):
                turn = l * NW + w
                act.wait_ge(s["projected"], turn + 1)
                act.wait_ge(s["table_written"], 48 * turn)
                act.activation(hs[0:C + 1, :], psH[0:C + 1, 0:WIN], ACT.Copy).then_inc(s["h_copied"], 1)
                act.activation(tabs[0:BLOCK, :, :], psTab[0:BLOCK, 0:BPW * EXT].rearrange("p (b c) -> p b c", b=BPW), ACT.Copy).then_inc(s["h_copied"], 1)

            def fast(l):
                own = Chain(act, own_sems["scalar", "fast", l])

                def indices(c, r):
                    if not exists(c):
                        return
                    q = l * NCH + c
                    act.wait_ge(s["turned"], q + 1)
                    since(act, "expanded", q - 2)
                    own.link(act.activation(c_dl[:, r, :, :], psT[:, CT:3 * CT].rearrange("p (k t) -> p k t", k=2), ACT.Copy))
                    act.activation(c_idx[:, r, :], psT[:, 0:CT], ACT.Copy).then_inc(s["idx_ready"], 1)

                def turn(c, r):
                    q = l * NCH + c
                    act.wait_ge(s["v_turned"], q + 1)
                    since(act, "vrow_in", 16 * q)
                    act.activation(t_v[0:CT, :], psH[0:CT, 0:P], ACT.Copy).then_inc(s["vt_ready"], 1)
                    indices(c + 2, (r + 2) % RING)
                    act.wait_ge(s["scored"], q + 1)
                    act.activation(fr[0:1, 3:4], fr[0:1, 2:3], ACT.Exp).then_inc(s["factor_ready"], 1)
                    own.link(act.activation(c_w[:, :], c_s[:, 1, :], ACT.Exp))
                    for t in range(CT):
                        last = act.activation(rows[:, r, t, 0:C + 1], rows[:, r, t, 0:C + 1], ACT.Copy, scale=c_w[:, t:t + 1])
                        if t % GT == GT - 1:
                            last.then_inc(s["scaled"], 1)

                indices(0, 0)
                indices(1, 1)
                over_chunks(act, turn, own, 2)

            def general(l):
                with act.Fori(0, TILES) as t:
                    act.wait_ge(g[l]["e_wt"], t + 1)
                    act.activation(g_c[:, 4:6], g_c[:, 2:4], ACT.Exp).then_inc(g[l]["e_exp"], 1)
                with act.Fori(0, NW) as w:
                    act.wait_ge(g[l]["gb_turned"], w + 1)
                    act.activation(acc[0:STATE, bass.ds(w * WIN, WIN)], psT[0:STATE, 0:WIN], ACT.Copy).then_inc(g[l]["gb_copied"], 1)

            def finish(l):
                with act.Fori(0, NW) as w:
                    turn = w + l * NW
                    act.wait_ge(s["delta_spread"], turn + 1)
                    act.wait_ge(s["total_ready"], turn)
                    act.activation(lin[0:C + 1, :], psD[0:C + 1, 0:WIN], ACT.Exp, scale=-1.0).then_inc(s["self_weight"], 1)
                act.wait_ge(s["norm_ready"], NW * (l + 1))
                act.activation(acc[0:C, 0:N], acc[0:C, 0:N], ACT.Identity, bias=gn[0:C, l:l + 1], accum_out=stat[0:C, 0:1]).then_inc(s["sum_ready"], 1)
                act.wait_ge(s["shift_ready"], l + 1)
                act.activation(big[0:C, 0:N], acc[0:C, 0:N], ACT.Square, bias=stat[0:C, 1:2], accum_out=stat[0:C, 2:3]).then_inc(s["square_ready"], 1)
                act.wait_ge(s["var_ready"], NW + l + 1)
                act.activation(stat[0:C, 4:5], stat[0:C, 3:4], ACT.Sqrt).then_inc(s["gn_std"], 1)
                act.wait_ge(s["gn_ready"], l + 1)

            own = Chain(act, s["own_scalar"])
            act.wait_ge(s["wt_psum"], 2)
            for l in range(2):
                act.activation(wext[0:C, l, 0:C], psT[0:C, l * C:(l + 1) * C], ACT.Copy).then_inc(s["wt_copied"], 1)
                act.activation(wext[0:C, l, C + 1:EXT], psT[0:C, 2 * C + 2 * l:2 * C + 2 * l + 2], ACT.Copy).then_inc(s["wt_copied"], 1)
            with act.Fori(0, NW) as w:
                act.wait_ge(s["var_ready"], w + 1)
                act.activation(xs[0:BLOCK, 2, :], xs[0:BLOCK, 1, :], ACT.Sqrt).then_inc(s["std_ready"], 1)
                act.wait_ge(s["xt_done"], w + 1)
                act.wait_ge(s["projected"], w)
                act.wait_ge(s["h0_stored"], 16 * w)
                act.activation(Y[0:C, :], psT[0:C, 0:WIN], ACT.Copy).then_inc(s["y_ready"], 1)
                copy_projection(0, w)
            act.wait_ge(s["flag_ready"], 1)
            unordered = act.value_load(flag[0:1, 0:1], min_val=0, max_val=1)
            by_order(act, unordered, fast, general, 0)
            finish(0)
            with act.Fori(0, NW) as w:
                act.wait_ge(s["y_ready"], w + NW)
                act.activation(lin[0:C, :], acc[0:C, bass.ds(w * WIN, WIN)], ACT.Identity, bias=stat[0:C, 6:7], scale=stat[0:C, 5:6]).then_inc(s["lin_ready"], 1)
                copy_projection(1, w)
            by_order(act, unordered, fast, general, 1)
            finish(1)
            with act.Fori(0, NW) as w:
                act.wait_ge(s["v_ready"], w)
                act.activation(lin[0:C, :], acc[0:C, bass.ds(w * WIN, WIN)], ACT.Identity, bias=stat[0:C, 6:7], scale=stat[0:C, 5:6]).then_inc(s["lin_ready"], 1)

        @block.tensor
        def _(pe):
            pe.wait_ge(s["consts_made"], 1)
            pe.wait_ge(s["weights_in"], 16 * 11)
            for l in range(2):
                pe.transpose(psT[0:C, l * C:(l + 1) * C], wraw[0:C, l, :], ident[0:C, 0:C])
                pe.matmul(psT[0:C, 2 * C + 2 * l:2 * C + 2 * l + 2], wraw[0:C, l, :], avec[0:C, 2 * l:2 * l + 2], start=True, stop=True).then_inc(s["wt_psum"], 1)
            pe.wait_ge(s["wt_copied"], 4)
            pe.wait_ge(s["first_row"], 1)
            for at in range(0, NG, 512):
                width = min(512, NG - at)
                last = pe.matmul([psD, psZ][at // 512][:, 0:width], ones[0:1, :], first_f[0:1, at:at + width], start=True, stop=True)
            last.then_inc(s["first_spread"], 1)
            pe.wait_ge(s["checked"], 1)
            pe.matmul(psE[0:1, 0:1], viol[0:NCH, 0:1], ones[0:NCH, 0:1], start=True, stop=True).then_inc(s["flag_psum"], 1)

            def project(l, w):
                turn = l * NW + w
                pe.wait_ge(s["y_ready"], turn + 1)
                pe.wait_ge(s["h_copied"], 2 * turn)
                pe.matmul(psH[0:C + 1, 0:WIN], wext[0:C + 1, l, 0:C + 1], Y[0:C + 1, :], start=True, stop=True)
                for b in range(BPW):
                    last = pe.matmul(psTab[0:BLOCK, b * EXT:(b + 1) * EXT], Y[0:C + 1, b * BLOCK:(b + 1) * BLOCK], wext[0:C + 1, l, :], start=True, stop=True)
                last.then_inc(s["projected"], 1)

            def fast(l):
                def turn_indices(c, r):
                    if not exists(c):
                        return
                    q = l * NCH + c
                    pe.wait_ge(s["prep_made"], q + 1)
                    since(pe, "idx_ready", q)
                    since(pe, "dl_ready", q)
                    pe.sem_inc(s["pe_passed"], 1)
                    for k in range(3):
                        last = pe.transpose(psT[:, k * CT:(k + 1) * CT], t_flt[0:CT, TRIO[r], k, :], ident[0:CT, 0:CT])
                    last.then_inc(s["turned"], 1)

                def turn(c, r):
                    q = l * NCH + c
                    pe.wait_ge(s["v_col"], q + 1)
                    since(pe, "vt_ready", q)
                    pe.transpose(psH[0:CT, 0:P], c_v[:, :], ident[:, :]).then_inc(s["v_turned"], 1)
                    turn_indices(c + 2, (r + 2) % RING)
                    pe.wait_ge(s["mrow_back"], 16 * (q + 1))
                    since(pe, "scored", q)
                    pe.sem_inc(s["pe_passed"], 1)
                    pe.transpose(psTab[:, 0:CT], t_m[0:CT, :], ident[0:CT, 0:CT]).then_inc(s["m_turned"], 1)
                    pe.wait_ge(s["factor_ready"], q + 1)
                    since(pe, "added", q)
                    pe.matmul(psU[0:C + 1, 0:1], ones[0:1, 0:C + 1], fr[0:1, 3:4], start=True, stop=True).then_inc(s["factor_spread"], 1)
                    for k in range(GROUPS):
                        pe.wait_ge(s["scaled"], GROUPS * q + k + 1)
                        for t in range(k * GT, (k + 1) * GT):
                            last = pe.matmul(psW[TRIO[r]][0:TAB, k * W:(k + 1) * W], rows[:, r, t, :], onehot[:, TRIO[r], t, :],
                                             start=(t % GT == 0), stop=(t % GT == GT - 1))
                    last.then_inc(s["summed"], 1)

                turn_indices(0, 0)
                turn_indices(1, 1)
                over_chunks(pe, turn)

            def general(l):
                with pe.Fori(0, TILES) as t:
                    pe.wait_ge(g[l]["e_diag"], t + 1)
                    pe.matmul(psE[:, 0:P], ones[:, :], g_diag[:, :], start=True, stop=True).then_inc(g[l]["e_row"], 1)
                    pe.wait_ge(g[l]["e_weighted"], t + 1)
                    pe.matmul(psU[:, 0:C + 1], g_eq[:, :], g_w[:, 0:C + 1], start=True, stop=True).then_inc(g[l]["e_sum"], 1)
                with pe.Fori(0, NW) as w:
                    turn = w
                    pe.wait_ge(g[l]["gb_ready"], turn + 1)
                    pe.wait_ge(g[l]["gb_copied"], turn)
                    for b in range(BPW):
                        last = pe.transpose(psT[0:STATE, b * BLOCK:(b + 1) * BLOCK], g_init[0:BLOCK, b, :], ident[0:BLOCK, 0:BLOCK])
                    last.then_inc(g[l]["gb_turned"], 1)

                pe.wait_ge(g[l]["gb_copied"], NW)

            def finish(l):
                with pe.Fori(0, NW) as w:
                    turn = w + l * NW
                    win = bass.ds(w * WIN, WIN)
                    pe.wait_ge(s["self_weight"], turn)
                    pe.matmul(psD[0:C + 1, 0:WIN], sel_delta[0:C + 2, 0:C + 1], acc[0:C + 2, win], start=True, stop=True).then_inc(s["delta_spread"], 1)
                    pe.wait_ge(s["total_ready"], turn + 1)
                    pe.wait_ge(s["norm_ready"], turn)
                    pe.matmul(psZ[0:C, 0:WIN], sel_z[0:C + 1, 0:C], acc[0:C + 1, win], start=True, stop=True).then_inc(s["z_spread"], 1)

            with pe.Fori(0, NW) as w:
                pe.wait_ge(s["xn_ready"], w + 1)
                pe.wait_ge(s["y_ready"], w)
                for b in range(BPW):
                    last = pe.transpose(psT[0:C, b * BLOCK:(b + 1) * BLOCK], xn[0:BLOCK, b, :], ident[0:BLOCK, 0:BLOCK])
                last.then_inc(s["xt_done"], 1)
                project(0, w)
            pe.wait_ge(s["flag_ready"], 1)
            unordered = pe.value_load(flag[0:1, 0:1], min_val=0, max_val=1)
            by_order(pe, unordered, fast, general, 0)
            finish(0)
            with pe.Fori(0, NW) as w:
                project(1, w)
            by_order(pe, unordered, fast, general, 1)
            finish(1)
            with pe.Fori(0, NW) as w:
                pe.wait_ge(s["v_ready"], w + 1)
                pe.wait_ge(s["out_ready"], w)
                for b in range(BPW):
                    last = pe.transpose(psTab[0:BLOCK, b * C:(b + 1) * C], Y[0:C, b * BLOCK:(b + 1) * BLOCK], ident[0:C, 0:C])
                last.then_inc(s["v_back"], 1)

        @block.vector
        def _(dve):
            own = Chain(dve, s["own_vector"])
            link = own.link

            def fast(l):
                own = Chain(dve, own_sems["vector", "fast", l])
                link = own.link

                def prepare(c, r):
                    if not exists(c):
                        return
                    q = l * NCH + c
                    b = TRIO[r]
                    dve.wait_ge(s["prep_in"], 64 * (q + 1))
                    since(dve, "turned", q - 1)
                    since(dve, "penrow_in", 16 * (q - 1))
                    link(dve.tensor_tensor(t_pen[0:CT, b, :], t_int[0:CT, b, 1, :], t_int[0:CT, b, 2, :], ALU.is_equal))
                    link(dve.tensor_scalar(t_pen[0:CT, b, :], t_pen[0:CT, b, :], -1.0, BIG, ALU.add, ALU.mult))
                    dve.tensor_tensor(t_flt[0:CT, b, 2, :], t_int[0:CT, b, 1, :], t_int[0:CT, b, 3, :], ALU.not_equal)
                    dve.tensor_copy(t_flt[0:CT, b, 0:2, :], t_int[0:CT, b, 0:2, :]).then_inc(s["prep_made"], 1)

                def localise(c, r):
                    if not exists(c):
                        return
                    q = l * NCH + c
                    dve.wait_ge(s["idx_ready"], q + 1)
                    dve.tensor_tensor(c_dl[:, r, 0, :].rearrange("p (g t) -> p g t", g=GROUPS), c_dl[:, r, 0, :].rearrange("p (g t) -> p g t", g=GROUPS),
                                      first_all[:, bass.ds(c * GROUPS, GROUPS)].unsqueeze(2).to_broadcast([P, GROUPS, GT]), ALU.subtract).then_inc(s["dl_ready"], 1)

                def expand(c, r):
                    if not exists(c):
                        return
                    q = l * NCH + c
                    b = TRIO[r]
                    since(dve, "summed", q - 1)
                    dve.wait_ge(s["dl_ready"], q + 1)
                    link(dve.tensor_tensor(onehot[:, b, :, :], iota[:, :].unsqueeze(1).to_broadcast([P, CT, W]),
                                           c_dl[:, r, 0, :].unsqueeze(2).to_broadcast([P, CT, W]), ALU.is_equal))
                    dve.wait_ge(s["awin_in"], 16 * GROUPS * (q + 1))
                    for k in range(2):
                        link(dve.tensor_tensor(prod[:, :, :].rearrange("p (g t) w -> p g t w", g=GROUPS),
                                               onehot[:, b, :, :].rearrange("p (g t) w -> p g t w", g=GROUPS),
                                               a_win[:, b, :, :, k].unsqueeze(2).to_broadcast([P, GROUPS, GT, W]), ALU.mult))
                        link(dve.tensor_reduce(c_own[:, r, k, :], prod[:, :, :], AX, ALU.add))
                    dve.sem_inc(s["expanded"], 1)

                def add_windows(c, r):
                    if not exists(c):
                        return
                    q = l * NCH + c
                    dve.wait_ge(s["summed"], q + 1)
                    dve.wait_ge(s["factor_spread"], q + 1)
                    for k in range(GROUPS):
                        first = dve.value_load(first_i[0:1, bass.ds(c * GROUPS + k, 1)], min_val=0, max_val=N - 1)
                        if k == 0:
                            link(dve.tensor_tensor(acc[0:C + 1, bass.ds(first, 1)], acc[0:C + 1, bass.ds(first, 1)], psU[0:C + 1, 0:1], ALU.mult))
                        link(dve.tensor_tensor(acc[0:TAB, bass.ds(first, W)], acc[0:TAB, bass.ds(first, W)],
                                               psW[TRIO[r]][0:TAB, k * W:(k + 1) * W], ALU.add))
                    dve.sem_inc(s["added"], 1)

                def turn(c, r):
                    q = l * NCH + c
                    dve.wait_ge(gathered[r], 16 * CT * (l * len(range(r, NCH, RING)) + (c - r) // RING + 1) if isinstance(c, int)
                                else (c - r) * (16 * CT // RING) + 16 * CT * (l * len(range(r, NCH, RING)) + 1))
                    dve.tensor_tensor(c_v[:, :], rows[:, r, :, C + 1], c_own[:, r, 0, :], ALU.max).then_inc(s["v_col"], 1)
                    prepare(c + 2, (r + 2) % RING)
                    localise(c + 2, (r + 2) % RING)
                    if not (isinstance(c, int) and c == 0):
                        add_windows(c - 1, (r - 1) % RING)
                    dve.wait_ge(s["vrow_in"], 16 * (q + 1))
                    dve.wait_ge(s["penrow_in"], 16 * (q + 1))
                    link(dve.tensor_copy(fr[0:1, 0:1], carry[0:1, :]))
                    link(dve.tensor_tensor_scan(row_v[0:1, :], row_pen[0:1, 0:CE], row_v[0:1, :], carry[0:1, 0:1], ALU.add, ALU.max))
                    link(dve.tensor_tensor_scan(row_v[0:1, ::-1], row_pen[0:1, CE:0:-1], row_v[0:1, ::-1], -BIG, ALU.add, ALU.max))
                    dve.tensor_copy(carry[0:1, :], row_v[0:1, CE - 1:CE])
                    link(dve.tensor_copy(fr[0:1, 1:2], row_v[0:1, 0:1]))
                    dve.sem_inc(s["scanned"], 1)
                    expand(c + 1, (r + 1) % RING)
                    own_r = c_own[:, r, :, :]
                    dve.tensor_tensor(c_q[:, 0, :], rows[:, r, :, C + 1], own_r[:, 1, :], ALU.add)
                    dve.tensor_tensor(c_q[:, 2, :], own_r[:, 0, :], own_r[:, 1, :], ALU.add)
                    link(dve.tensor_tensor(fr[0:1, 0:2], fr[0:1, 0:2], c_own[0:1, r, 1, 0:1].to_broadcast([1, 2]), ALU.add))
                    link(dve.scalar_tensor_tensor(out=fr[0:1, 0:2], in0=fr[0:1, 0:2], scalar=SLOPE_ATT, in1=fr[0:1, 0:2], op0=ALU.mult, op1=ALU.max))
                    link(dve.tensor_scalar(fr[0:1, 2:3], fr[0:1, 0:1], fr[0:1, 1:2], 0.0, ALU.subtract, ALU.min))
                    dve.wait_ge(s["m_turned"], q + 1)
                    link(dve.tensor_tensor(c_q[:, 1, :], psTab[:, 0:CT], own_r[:, 1, :], ALU.add))
                    link(dve.scalar_tensor_tensor(out=c_q[:, :, :], in0=c_q[:, :, :], scalar=SLOPE_ATT, in1=c_q[:, :, :], op0=ALU.mult, op1=ALU.max))
                    dve.tensor_tensor(c_s[:, 1, :], c_q[:, 0, :], c_q[:, 1, :], ALU.subtract)
                    link(dve.tensor_tensor(c_s[:, 0, :], c_q[:, 1, :], c_q[:, 2, :], ALU.subtract))
                    dve.tensor_tensor(rows[:, r, :, C + 1], c_s[:, 0, :], c_dl[:, r, 1, :], ALU.mult).then_inc(s["scored"], 1)

                link(dve.memset(carry[0:1, :], -BIG))
                for c in range(2):
                    prepare(c, c)
                    localise(c, c)
                expand(0, 0)
                over_chunks(dve, turn, own, 23)
                add_windows(NCH - 1, (NCH - 1) % RING)

            def general(l):
                own = Chain(dve, own_sems["vector", "general", l])
                link = own.link
                with dve.Fori(0, NW) as w:
                    turn = w
                    own.enter(w, 2)
                    dve.wait_ge(g[l]["gi_in"], 32 * turn + 32)
                    link(dve.tensor_tensor(xs[0:BLOCK, 0, :], g_alph[0:BLOCK, :, 0], g_alph[0:BLOCK, :, 1], ALU.add))
                    link(dve.tensor_copy(g_init[0:BLOCK, :, C + 2:C + 3], g_alph[0:BLOCK, :, 1:2]))
                    dve.scalar_tensor_tensor(out=g_init[0:BLOCK, :, C + 1], in0=xs[0:BLOCK, 0, :], scalar=SLOPE_ATT, in1=xs[0:BLOCK, 0, :],
                                             op0=ALU.mult, op1=ALU.max).then_inc(g[l]["gi_ready"], 1)
                own.leave(NW)
                with dve.Fori(0, TILES) as t:
                    own.enter(t, 12)
                    dve.wait_ge(g[l]["e_dst"], 16 * t + 16)
                    dve.wait_ge(g[l]["e_dstrow"], 16 * t + 16)
                    dve.wait_ge(g[l]["e_scattered"], 16 * t)
                    link(dve.tensor_copy(g_c[:, 0:1], g_dst[:, :]))
                    link(dve.tensor_copy(g_tmp[:, :], g_dstrow[:, :]))
                    link(dve.tensor_scalar(g_eq[:, :], g_tmp[:, :], g_c[:, 0:1], None, ALU.is_equal))
                    link(dve.tensor_tensor(g_tmp[:, :], g_eq[:, :], lower[:, :], ALU.mult))
                    link(dve.tensor_reduce(g_c[:, 1:2], g_tmp[:, :], AX, ALU.add))
                    dve.scalar_tensor_tensor(out=g_sidx[:, :], in0=g_c[:, 1:2], scalar=1e6, in1=g_c[:, 0:1], op0=ALU.mult, op1=ALU.add)
                    dve.wait_ge(g[l]["e_rows"], 16 * t + 16)
                    dve.wait_ge(g[l]["e_old"], 16 * t + 16)
                    link(dve.tensor_tensor(g_c[:, 6:7], g_rows[:, C + 1:C + 2], g_old[:, C + 2:C + 3], ALU.add))
                    link(dve.scalar_tensor_tensor(out=g_c[:, 1:2], in0=g_c[:, 6:7], scalar=SLOPE_ATT, in1=g_c[:, 6:7], op0=ALU.mult, op1=ALU.max))
                    dve.tensor_scalar(g_diag[:, :], ident[:, :], g_c[:, 1:2], None, ALU.mult).then_inc(g[l]["e_diag"], 1)
                    link(dve.tensor_scalar(g_tmp[:, :], g_eq[:, :], BIG, -BIG, ALU.mult, ALU.add))
                    dve.wait_ge(g[l]["e_row"], t + 1)
                    link(dve.tensor_tensor(g_tmp[:, :], g_tmp[:, :], psE[:, 0:P], ALU.add))
                    link(dve.tensor_reduce(g_c[:, 6:7], g_tmp[:, :], AX, ALU.max))
                    link(dve.tensor_tensor(g_new[:, C + 1:C + 2], g_c[:, 6:7], g_old[:, C + 1:C + 2], ALU.max))
                    dve.tensor_tensor(g_c[:, 2:3], g_old[:, C + 1:C + 2], g_new[:, C + 1:C + 2], ALU.subtract)
                    link(dve.tensor_tensor(g_c[:, 3:4], g_c[:, 1:2], g_new[:, C + 1:C + 2], ALU.subtract))
                    dve.tensor_copy(g_new[:, C + 2:C + 3], g_old[:, C + 2:C + 3]).then_inc(g[l]["e_wt"], 1)
                    dve.wait_ge(g[l]["e_exp"], t + 1)
                    dve.tensor_scalar(g_w[:, 0:C + 1], g_rows[:, 0:C + 1], g_c[:, 5:6], None, ALU.mult).then_inc(g[l]["e_weighted"], 1)
                    dve.wait_ge(g[l]["e_sum"], t + 1)
                    dve.scalar_tensor_tensor(out=g_new[:, 0:C + 1], in0=g_old[:, 0:C + 1], scalar=g_c[:, 4:5], in1=psU[:, 0:C + 1],
                                             op0=ALU.mult, op1=ALU.add).then_inc(g[l]["e_new"], 1)
                own.leave(TILES)
                with dve.Fori(0, NW) as w:
                    dve.wait_ge(g[l]["gb_in"], 16 * w + 16)
                    dve.memset(g_init[0:BLOCK, :, C + 1:C + 2], 1e4).then_inc(g[l]["gb_ready"], 1)

            def finish(l):
                with dve.Fori(0, NW) as w:
                    turn = w + l * NW
                    win = bass.ds(w * WIN, WIN)
                    own.enter(w, 2)
                    dve.wait_ge(s["self_weight"], turn + 1)
                    dve.wait_ge(s["h_in"], 16 * (turn + 1))
                    link(dve.tensor_tensor(lin[0:C + 1, :], lin[0:C + 1, :], hs[0:C + 1, :], ALU.mult))
                    dve.tensor_tensor(acc[0:C + 1, win], acc[0:C + 1, win], lin[0:C + 1, :], ALU.add).then_inc(s["total_ready"], 1)
                    dve.wait_ge(s["z_spread"], turn + 1)
                    link(dve.reciprocal(res[0:C, :], psZ[0:C, 0:WIN]))
                    dve.tensor_tensor(acc[0:C, win], acc[0:C, win], res[0:C, :], ALU.mult).then_inc(s["norm_ready"], 1)
                own.leave(NW)
                dve.wait_ge(s["sum_ready"], l + 1)
                link(dve.tensor_scalar(stat[0:C, 7:8], stat[0:C, 0:1], -1.0 / N, None, ALU.mult))
                dve.tensor_tensor(stat[0:C, 1:2], stat[0:C, 7:8], gn[0:C, 4:5], ALU.mult).then_inc(s["shift_ready"], 1)
                dve.wait_ge(s["square_ready"], l + 1)
                dve.tensor_scalar(stat[0:C, 3:4], stat[0:C, 2:3], 1.0 / N, EPS, ALU.mult, ALU.add).then_inc(s["var_ready"], 1)
                dve.wait_ge(s["gn_std"], l + 1)
                link(dve.reciprocal(stat[0:C, 7:8], stat[0:C, 4:5]))
                link(dve.tensor_tensor(stat[0:C, 5:6], stat[0:C, 7:8], gn[0:C, 2:3], ALU.mult))
                link(dve.tensor_tensor(stat[0:C, 7:8], stat[0:C, 5:6], stat[0:C, 1:2], ALU.mult))
                dve.tensor_tensor(stat[0:C, 6:7], stat[0:C, 7:8], gn[0:C, 3:4], ALU.add).then_inc(s["gn_ready"], 1)

            dve.wait_ge(s["firsts_in"], 32)
            dve.tensor_copy(last_f[0:1, :], last_i[0:1, :])
            link(dve.tensor_copy(first_f[0:1, :], first_i[0:1, :]))
            dve.sem_inc(s["first_row"], 1)
            link(dve.tensor_tensor(last_f[0:1, :], last_f[0:1, :], first_f[0:1, :], ALU.subtract))
            link(dve.tensor_scalar(last_f[0:1, :], last_f[0:1, :], float(W), None, ALU.is_ge))
            link(dve.tensor_reduce(viol[0:1, 1:2], last_f[0:1, :], AX, ALU.add))
            dve.wait_ge(s["check_in"], 32)
            link(dve.tensor_tensor(big[0:NCH, 0:CE], big[0:NCH, 0:CE].bitcast(I32), big[0:NCH, CE:2 * CE].bitcast(I32), ALU.is_gt))
            link(dve.tensor_reduce(viol[0:NCH, 0:1], big[0:NCH, 0:CE], AX, ALU.add))
            dve.sem_inc(s["checked"], 1)
            dve.wait_ge(s["flag_psum"], 1)
            link(dve.tensor_tensor(viol[0:1, 2:3], psE[0:1, 0:1], viol[0:1, 1:2], ALU.add))
            link(dve.tensor_scalar(flag[0:1, :], viol[0:1, 2:3], 0.5, None, ALU.is_ge))
            dve.sem_inc(s["flag_ready"], 1)
            dve.wait_ge(s["first_spread"], 1)
            for at in range(0, NG, 512):
                width = min(512, NG - at)
                link(dve.tensor_copy(first_all[:, at:at + width], [psD, psZ][at // 512][:, 0:width]))
            with dve.Fori(0, NW) as w:
                own.enter(w, 6)
                dve.wait_ge(s["x_in"], 16 * w + 16)
                link(dve.tensor_reduce(xs[0:BLOCK, 0, :], xin[0:BLOCK, :, :], AX, ALU.add))
                link(dve.tensor_scalar(xs[0:BLOCK, 3, :], xs[0:BLOCK, 0, :], 1.0 / C, None, ALU.mult))
                link(dve.tensor_tensor(xc[0:BLOCK, :, :], xin[0:BLOCK, :, :], xs[0:BLOCK, 3, :].unsqueeze(2).to_broadcast([BLOCK, BPW, C]), ALU.subtract))
                dve.wait_ge(s["xt_done"], w)
                link(dve.tensor_tensor(xn[0:BLOCK, :, :], xc[0:BLOCK, :, :], xc[0:BLOCK, :, :], ALU.mult))
                link(dve.tensor_reduce(xs[0:BLOCK, 0, :], xn[0:BLOCK, :, :], AX, ALU.add))
                dve.tensor_scalar(xs[0:BLOCK, 1, :], xs[0:BLOCK, 0, :], 1.0 / C, EPS, ALU.mult, ALU.add).then_inc(s["var_ready"], 1)
                dve.wait_ge(s["std_ready"], w + 1)
                link(dve.reciprocal(xs[0:BLOCK, 3, :], xs[0:BLOCK, 2, :]))
                dve.scalar_tensor_tensor(out=xn[0:BLOCK, :, :], in0=xc[0:BLOCK, :, :], scalar=0.0,
                                         in1=xs[0:BLOCK, 3, :].unsqueeze(2).to_broadcast([BLOCK, BPW, C]), op0=ALU.max, op1=ALU.mult).then_inc(s["xn_ready"], 1)
            own.leave(NW)
            dve.wait_ge(s["flag_ready"], 1)
            unordered = dve.value_load(flag[0:1, 0:1], min_val=0, max_val=1)
            by_order(dve, unordered, fast, general, 0)
            finish(0)
            with dve.Fori(0, NW) as w:
                dve.wait_ge(s["lin_ready"], w + 1)
                dve.tensor_copy(acc[0:TAB, bass.ds(w * WIN, WIN)], zeros[0:TAB, :])
                dve.wait_ge(s["projected"], w + NW)
                dve.scalar_tensor_tensor(out=Y[0:C, :], in0=lin[0:C, :], scalar=SLOPE_ACT, in1=lin[0:C, :], op0=ALU.mult, op1=ALU.max).then_inc(s["y_ready"], 1)
            by_order(dve, unordered, fast, general, 1)
            finish(1)
            with dve.Fori(0, NW) as w:
                own.enter(w, 1)
                dve.wait_ge(s["lin_ready"], w + NW + 1)
                dve.wait_ge(s["res_in"], 16 * w + 16)
                link(dve.tensor_tensor(res[0:C, :], lin[0:C, :], res[0:C, :], ALU.add))
                dve.scalar_tensor_tensor(out=Y[0:C, :], in0=res[0:C, :], scalar=SLOPE_ACT, in1=res[0:C, :], op0=ALU.mult, op1=ALU.max).then_inc(s["v_ready"], 1)
                dve.wait_ge(s["v_back"], w + 1)
                dve.wait_ge(s["x_in"], 16 * (w + NW) + 16)
                dve.wait_ge(s["out_written"], 16 * w)
                dve.tensor_tensor(xn[0:BLOCK, :, :], psTab[0:BLOCK, 0:BPW * C].rearrange("p (b c) -> p b c", b=BPW), xin[0:BLOCK, :, :], ALU.add).then_inc(s["out_ready"], 1)
            own.leave(NW)


_INS = ["x", "src", "dst", "L0_gnn_W1", "L0_gnn_att_src1", "L0_gnn_att_dst1", "L0_gnn_b1", "L0_gnn_W2", "L0_gnn_att_src2",
        "L0_gnn_att_dst2", "L0_gnn_b2", "L0_gnn_gn_weight", "L0_gnn_gn_bias", "L0_gnn_gn_mean_scale"]


def kernel(**inputs):
    import numpy as _np
    import concourse.bacc as _bacc
    from concourse import mybir as _mybir
    from concourse.bass_utils import run_bass_kernel_spmd as _run

    nc = _bacc.Bacc("TRN2", target_bir_lowering=False, num_devices=1)
    arrays, args = {}, []
    for name in _INS:
        a = _np.ascontiguousarray(inputs[name])
        arrays[f"in_{name}_dram"] = a
        args.append(nc.dram_tensor(f"in_{name}_dram", a.shape, _mybir.dt.from_np(a.dtype), kind="ExternalInput").ap())
    args.append(nc.dram_tensor("out_0_dram", inputs["x"].shape, _mybir.dt.float32, kind="ExternalOutput").ap())
    gat_kernel(nc, *args)
    r = _run(nc, [arrays], core_ids=[0])
    return r.results[0]["out_0_dram"]
```

```python
from contextlib import ExitStack

import concourse.bass as bass
from concourse import mybir

P = 128
C = 96
BLOCK = 125
BPW = 4
WIN = BLOCK * BPW
ROW = C + 3
SUMS = C + 2
STATE = C + 3
SLOPE_ATT = 0.2
SLOPE_ACT = 0.01
EPS = 1e-5
BIG = 1e30
RING = 4
PAIR = [0, 1, 0, 1]
CT = 25
GT = 5
GROUPS = CT // GT
PARTS = 3
W = 64
CE = CT * P
TURNED = 4
TURNS = -(-CT // TURNED)
TURN_BANKS = 3
M_TURN = 5
X_LOAD = 5

ALU = mybir.AluOpType
ACT = mybir.ActivationFunctionType
F32 = mybir.dt.float32
I32 = mybir.dt.int32
BF16 = mybir.dt.bfloat16
AX = mybir.AxisListType.X


class Chain:

    def __init__(self, eng, sem):
        self.eng, self.sem, self.n, self.turn = eng, sem, 0, 0

    def start(self, ins):
        ins.then_inc(self.sem, 1)
        self.n += 1

    def settle(self):
        self.eng.wait_ge(self.sem, self.turn + self.n)

    def link(self, ins):
        self.start(ins)
        self.settle()

    def enter(self, i, per):
        self.per, self.first, self.turn = per, self.n, i * per

    def leave(self, count):
        assert self.n - self.first == self.per, (self.n - self.first, self.per)
        self.turn, self.n = 0, self.first + self.per * count


def last_use(k):
    return k - TURN_BANKS if k >= TURN_BANKS else max(range(k, TURNS, TURN_BANKS)) - TURNS


def gat_kernel(nc, x, src, dst, W1, as1, ad1, b1, W2, as2, ad2, b2, gn_w, gn_b, gn_ms, out):
    N = x.shape[0]
    E = src.shape[0]
    NW = N // WIN
    TILES = E // P
    NCH = TILES // CT
    NG = NCH * GROUPS
    assert N % WIN == 0 and E % P == 0 and x.shape[1] == C
    assert TILES % CT == 0 and NCH <= P

    with ExitStack() as ctx:
        def sb(name, shape, dt=F32):
            return ctx.enter_context(nc.sbuf_tensor(name, shape, dt))

        def sem(name):
            return ctx.enter_context(nc.semaphore(name))

        def dram(name, shape, dt=F32):
            return nc.dram_tensor(name, shape, dt, kind="Internal").ap()

        table = dram("table", [N + W, ROW])
        y_d = [dram(f"y_d{l}", [C, N]) for l in range(2)]
        state = dram("state", [N, STATE])
        dst_pad = dram("dst_pad", [E + 2], I32)

        BXW = BPW * C
        acc = sb("acc", [P, N + W])
        big = sb("big", [P, max(NW * BXW, N, RING * CT * ROW)])
        rows = big[:, 0:RING * CT * ROW].rearrange("p (r t c) -> p r t c", r=RING, t=CT)
        z_rows = big[:, 0:N].bitcast(BF16).rearrange("p (z n) -> p z n", z=2)
        ident = sb("ident", [P, P])
        ones = sb("ones", [P, P])
        lower = sb("lower", [P, P])
        zeros = sb("zeros", [P, P])
        ones_b = sb("ones_b", [P, P], BF16)
        iota = sb("iota", [P, W])
        iota_i = sb("iota_i", [P, W], I32)
        minus = sb("minus", [P, 2], I32)
        wraw = sb("wraw", [P, 2, C])
        avec = sb("avec", [P, 4])
        wext = sb("wext", [P, 2, ROW])
        gn = sb("gn", [P, 5])
        stat = sb("stat", [P, 12])
        z_col = sb("z_col", [P, 2, N // BLOCK])
        z_rest = sb("z_rest", [P, 2, N // BLOCK])
        z_parts = sb("z_parts", [P, PARTS, 2, N // BLOCK], BF16)
        win_sum = sb("win_sum", [P, 2, NW])
        xs = sb("xs", [P, 4, NW * BPW])
        first_i = sb("first_i", [P, NG], I32)
        last_i = sb("last_i", [P, NG], I32)
        first_f = sb("first_f", [P, NG])
        last_f = sb("last_f", [P, NG])
        first_all = sb("first_all", [P, NG])
        viol = sb("viol", [P, 4])
        flag = sb("flag", [P, 1], I32)
        t_int = sb("t_int", [P, RING, 4, P], I32)
        t_flt = sb("t_flt", [P, RING, 3, P])
        t_pen = sb("t_pen", [P, RING, P])
        t_v = sb("t_v", [P, P])
        t_m = sb("t_m", [P, P])
        row_v = sb("row_v", [P, CE])
        row_pen = sb("row_pen", [P, CE + 1])
        carry = sb("carry", [P, 1])
        fr = sb("fr", [P, 4])
        c_idx = sb("c_idx", [P, RING, CT], I32)
        c_dl = sb("c_dl", [P, RING, 2, CT])
        c_own = sb("c_own", [P, RING, CT, 2])
        c_v = sb("c_v", [P, CT])
        c_q = sb("c_q", [P, 3, CT])
        c_s = sb("c_s", [P, 2, CT])
        c_w = sb("c_w", [P, 2, CT])
        a_win = sb("a_win", [P, RING, GROUPS, 2])
        a_rest = sb("a_rest", [P, GROUPS, 2])
        a_parts = sb("a_parts", [P, RING, GROUPS, PARTS, 2], BF16)
        g_src = sb("g_src", [P, 1], I32)
        g_dst = sb("g_dst", [P, 1], I32)
        g_dstrow = sb("g_dstrow", [P, P], I32)
        g_sidx = sb("g_sidx", [P, 1], I32)

        def parts(base, *widths):
            at, found = 0, []
            for width in widths:
                found.append(base[:, at:at + width])
                at += width
            return found

        room = sb("room", [P, RING * CT * W])
        onehot = room[:, :].rearrange("p (b t w) -> p b t w", b=RING, t=CT)
        Y, tabs, xn = parts(room, RING * WIN, RING * BPW * ROW, RING * BXW)
        Y = Y.rearrange("p (b n) -> p b n", b=RING)
        tabs = tabs.rearrange("p (b k c) -> p b k c", b=RING, k=BPW)
        xn = xn.rearrange("p (b k c) -> p b k c", b=RING, k=BPW)
        _, res, xout = parts(room, RING * WIN, RING * WIN, RING * BXW)
        res = res.rearrange("p (b n) -> p b n", b=RING)
        xout = xout.rearrange("p (b k c) -> p b k c", b=RING, k=BPW)
        squares = room[:, RING * WIN:RING * WIN + 2 * X_LOAD * BXW]
        junk = room[:, RING * WIN:(RING + 2) * WIN].rearrange("p (b n) -> p b n", b=2)
        side = sb("side", [P, RING * WIN])
        lin = side[:, :].rearrange("p (b n) -> p b n", b=RING)
        onehot_t = side[:, 0:TURN_BANKS * TURNED * P // 2].bitcast(BF16).rearrange("p (b n) -> p b n", b=TURN_BANKS)
        g_rows, g_old, g_new, g_eq, g_tmp, g_diag, g_w, g_c, g_init, g_alph = parts(
            side, ROW, STATE, STATE, P, P, P, C + 1, 8, BPW * STATE, BPW)
        g_init = g_init.rearrange("p (b c) -> p b c", b=BPW)

        psT, psH, psTab, psD, psZ, psE, psU, psX = [ctx.enter_context(nc.psum_tensor(f"bank{n}", [P, 512], F32)) for n in range(8)]
        bank_turn = [psT, psX]
        bank_rows = [psTab, psH, psU, psE]
        bank_tab = [psTab, psH]
        bank_z = [psD, psZ]
        bank_sum = [psD, psZ]
        bank_own = [psX, psU, psE]
        FACTOR = GROUPS * W

        names = """weights_in consts_made own_vector own_scalar own_pool pool_passed sp_passed pe_passed act_passed
        pad_written firsts_in first_row first_spread check_in check_done centred square_used edges_done flag_psum flag_ready
        wt_psum wt_copied square_made var_ready std_ready acc_clear
        xn_ready xt_done y_ready projected tab_copied
        z_moved self_weight z_split z_back z_spread z_copied h_spread both_made norm_ready biased square_ready gn_var gn_std gn_ready
        lin_ready v_ready v_back out_ready
        prep_in prep_made turned idx_ready dl_ready expanded onehot_turned onehot_copied awin_split own_psum own_ready
        v_col v_turned vt_ready vrow_in penrow_in scanned mrow_back m_turned
        scored factor_ready scaled summed added"""
        s = {k: sem(k) for k in names.split()}
        ring = {k: [sem(f"{k}_{r}") for r in range(RING)] for k in
                "x_in table_written y_written y_in awin_in gathered".split()}
        x_loaded = [sem(f"x_loaded_{k}") for k in range(-(-NW // X_LOAD))]
        own_sems = {(e, path, l): sem(f"own_{e}_{path}_{l}") for e, path in (("vector", "fast"), ("vector", "general"), ("scalar", "fast")) for l in range(2)}
        edge_names = """gi_in gi_ready gi_written e_src e_dst e_dstrow e_rows e_old e_new e_scattered e_diag e_row e_wt e_exp e_weighted e_sum
        gb_in gb_ready gb_turned gb_copied"""
        g = [{k: sem(f"{k}_{l}") for k in edge_names.split()} for l in range(2)]

        def since(eng, sem_, value):
            if not isinstance(value, int) or value > 0:
                eng.wait_ge(s[sem_] if isinstance(sem_, str) else sem_, value)

        def over(eng, count, turn, chain=None, per_round=0):
            if count <= 2 * RING:
                for c in range(count):
                    turn(c // RING, c % RING)
                return
            rounds = count // RING
            for r in range(RING):
                turn(0, r)
            with eng.Fori(1, rounds - 1) as i:
                if chain:
                    chain.enter(i - 1, per_round)
                for r in range(RING):
                    turn(i, r)
            if chain:
                chain.leave(rounds - 2)
            for c in range((rounds - 1) * RING, count):
                turn(c // RING, c % RING)

        def exists(count, i, r):
            return not isinstance(i, int) or 0 <= i * RING + r < count

        def step(i, r, k):
            return i + (r + k) // RING, (r + k) % RING

        def rounds_of(count, l, i, r):
            return i + 1 + l * len(range(r, count, RING))

        def all_landed(eng, name, count, passes):
            for r in range(min(RING, count)):
                eng.wait_ge(ring[name][r], 16 * passes * len(range(r, count, RING)))

        def edges(eng, unordered, fast, general, l):
            with eng.If(unordered < 1):
                fast(l)
            with eng.Else():
                general(l)

        def window_starts(engine, c):
            _, starts = nc.values_load_multi_w_load_instructions(
                first_i[0:1, bass.ds(c * GROUPS, GROUPS)], engines=(engine,), min_val=0, max_val=N - 1)
            return starts

        def of_window(ap, w):
            return ap[bass.ds(w * WIN, WIN), :].rearrange("(p b) c -> p b c", b=BPW)

        def cols(w):
            return bass.ds(w * WIN, WIN)

        x_loads = [(w, min(X_LOAD, NW - w)) for w in range(0, NW, X_LOAD)]

        block = ctx.enter_context(nc.Block())

        @block.sync
        def _(sp):
            def passed():
                sp.sem_inc(s["sp_passed"], 1)

            for k, (w, n) in enumerate(x_loads):
                sp.dma_start(big[0:BLOCK, w * BXW:(w + n) * BXW].rearrange("p (w c) -> p w c", c=BXW),
                             x[w * WIN:(w + n) * WIN, :].rearrange("(w p b) c -> p w (b c)", p=BLOCK, b=BPW)).then_inc(x_loaded[k], 16)

            def column(ap):
                return ap.rearrange("(c a) -> c a", a=1)

            for to, of in ((wraw[0:C, 0, :], W1), (wraw[0:C, 1, :], W2),
                           (avec[0:C, 0:1], column(as1)), (avec[0:C, 1:2], column(ad1)),
                           (avec[0:C, 2:3], column(as2)), (avec[0:C, 3:4], column(ad2)),
                           (gn[0:C, 0:1], column(b1)), (gn[0:C, 1:2], column(b2)),
                           (gn[0:C, 2:3], column(gn_w)), (gn[0:C, 3:4], column(gn_b)), (gn[0:C, 4:5], column(gn_ms))):
                sp.dma_start(to, of).then_inc(s["weights_in"], 16)
            by_group = dst.rearrange("(g a) -> a g", a=GT * P)
            sp.dma_start(first_i[0:1, :], by_group[0:1, :], allow_slow_non_contiguous=True).then_inc(s["firsts_in"], 16)
            sp.dma_start(last_i[0:1, :], by_group[GT * P - 1:GT * P, :], allow_slow_non_contiguous=True).then_inc(s["firsts_in"], 16)
            sp.wait_ge(s["consts_made"], 1)
            sp.dma_start(dst_pad[1:E + 1].rearrange("(p a) -> p a", p=P), dst.rearrange("(p a) -> p a", p=P)).then_inc(s["pad_written"], 16)
            sp.dma_start(dst_pad[0:1].rearrange("(p a) -> p a", p=1), minus[0:1, 0:1]).then_inc(s["pad_written"], 16)
            sp.dma_start(dst_pad[E + 1:E + 2].rearrange("(p a) -> p a", p=1), minus[0:1, 1:2]).then_inc(s["pad_written"], 16)
            sp.dma_start(table[N:N + W, :], zeros[0:W, 0:ROW]).then_inc(s["pad_written"], 16)
            sp.wait_ge(s["pad_written"], 64)
            sp.dma_start(row_v[0:NCH, :].bitcast(I32), dst_pad[0:E].rearrange("(c e) -> c e", e=CE)).then_inc(s["check_in"], 16)
            sp.dma_start(row_pen[0:NCH, 0:CE].bitcast(I32), dst_pad[1:E + 1].rearrange("(c e) -> c e", e=CE)).then_inc(s["check_in"], 16)

            def store_windows(l):
                def turn(i, r):
                    w = i * RING + r
                    sp.wait_ge(s["y_ready"], l * NW + w + 1)
                    passed()
                    sp.dma_start(y_d[l][:, cols(w)], Y[0:C, r, :]).then_inc(ring["y_written"][r], 16)
                    sp.wait_ge(s["tab_copied"], l * NW + w + 1)
                    passed()
                    sp.dma_start(of_window(table, w), tabs[0:BLOCK, r, :, :]).then_inc(ring["table_written"][r], 16)

                over(sp, NW, turn)

            def fast(l):
                def load_indices(i, r):
                    if not exists(NCH, i, r):
                        return
                    c = i * RING + r
                    q = l * NCH + c
                    since(sp, "prep_made", q)
                    passed()
                    for k, (ap, shift) in enumerate(((src, 0), (dst_pad, 1), (dst_pad, 0), (dst_pad, 2))):
                        sp.dma_start(t_int[0:CT, r, k, :], ap[bass.ds(c * CE + shift, CE)].rearrange("(t p) -> t p", p=P)).then_inc(s["prep_in"], 16)

                def load_windows(i, r):
                    if not exists(NCH, i, r):
                        return
                    c = i * RING + r
                    starts = window_starts(mybir.EngineType.SP, c)
                    since(sp, "awin_split", l * NCH + c + 1 - RING)
                    passed()
                    for k, first in enumerate(starts):
                        sp.dma_start(a_win[0:W, r, k, :], table[bass.ds(first, W), C + 1:ROW]).then_inc(ring["awin_in"][r], 16)

                def penalties(i, r):
                    if not exists(NCH, i, r):
                        return
                    q = l * NCH + i * RING + r
                    since(sp, "scanned", q)
                    passed()
                    sp.wait_ge(s["prep_made"], q + 1)
                    passed()
                    sp.dma_start(row_pen[0:1, 0:CE], t_pen[0:CT, r, :]).then_inc(s["penrow_in"], 16)

                def turn(i, r):
                    q = l * NCH + i * RING + r
                    sp.wait_ge(s["vt_ready"], q + 1)
                    passed()
                    sp.dma_start(row_v[0:1, :], t_v[0:CT, :]).then_inc(s["vrow_in"], 16)
                    load_indices(*step(i, r, 3))
                    load_windows(*step(i, r, 2))
                    since(sp, "m_turned", q)
                    passed()
                    sp.wait_ge(s["scanned"], q + 1)
                    passed()
                    sp.dma_start(t_m[0:CT, :], row_v[0:1, :]).then_inc(s["mrow_back"], 16)
                    penalties(*step(i, r, 1))

                for c in range(3):
                    load_indices(0, c)
                penalties(0, 0)
                all_landed(sp, "table_written", NW, l + 1)
                for c in range(2):
                    load_windows(0, c)
                over(sp, NCH, turn)

            def general(l):
                all_landed(sp, "table_written", NW, l + 1)

                def make_state(w):
                    since(sp, g[l]["gi_written"], 16 * w)
                    passed()
                    sp.dma_start(g_init[0:BLOCK, :, :], of_window(table, w)).then_inc(g[l]["gi_in"], 16)
                    sp.wait_ge(g[l]["gi_ready"], w + 1)
                    passed()
                    sp.dma_start(of_window(state, w), g_init[0:BLOCK, :, :]).then_inc(g[l]["gi_written"], 16)

                make_state(0)
                with sp.Fori(1, NW) as w:
                    make_state(w)

                def tile(t):
                    since(sp, g[l]["e_scattered"], 16 * t)
                    passed()
                    sp.dma_start(g_src[:, :], src[bass.ds(t * P, P)].rearrange("(p a) -> p a", a=1)).then_inc(g[l]["e_src"], 16)
                    sp.dma_start(g_dst[:, :], dst[bass.ds(t * P, P)].rearrange("(p a) -> p a", a=1)).then_inc(g[l]["e_dst"], 16)
                    sp.dma_start(g_dstrow[:, :], dst[bass.ds(t * P, P)].rearrange("(a p) -> a p", a=1).to_broadcast([P, P])).then_inc(g[l]["e_dstrow"], 16)

                tile(0)
                with sp.Fori(1, TILES) as t:
                    tile(t)
                sp.wait_ge(g[l]["e_scattered"], 16 * TILES)

                def read_state(w):
                    since(sp, g[l]["gb_turned"], w)
                    passed()
                    sp.dma_start(g_init[0:BLOCK, :, :], of_window(state, w)).then_inc(g[l]["gb_in"], 16)

                read_state(0)
                with sp.Fori(1, NW) as w:
                    read_state(w)
                sp.wait_ge(g[l]["gb_copied"], NW)

            def load_inputs(l):
                all_landed(sp, "y_written", NW, l + 1)
                sp.wait_ge(s["edges_done"], l + 1)

                for row in range(2):
                    sp.dma_start(z_col[0:BLOCK, row, :], acc[C + row:C + row + 1, 0:N]).then_inc(s["z_moved"], 16)

                def load(i, r):
                    if not exists(NW, i, r):
                        return
                    w = i * RING + r
                    since(sp, "h_spread", l * NW + w + 1 - RING)
                    passed()
                    sp.dma_start(Y[0:C, r, :], y_d[l][:, cols(w)]).then_inc(ring["y_in"][r], 16)

                for r in range(RING):
                    load(0, r)
                sp.wait_ge(s["z_split"], l + 1)
                for k in range(PARTS):
                    for z in range(2):
                        sp.dma_start(z_rows[k:k + 1, z, :], z_parts[0:BLOCK, k, z, :]).then_inc(s["z_back"], 16)
                over(sp, NW, lambda i, r: load(*step(i, r, RING)))

            store_windows(0)
            sp.wait_ge(s["flag_ready"], 1)
            unordered = sp.value_load(flag[0:1, 0:1], min_val=0, max_val=1)
            edges(sp, unordered, fast, general, 0)
            load_inputs(0)
            store_windows(1)
            edges(sp, unordered, fast, general, 1)
            load_inputs(1)

            sp.wait_ge(s["gn_ready"], 2)

            def load_last(i, r):
                w = i * RING + r
                since(sp, "v_ready", w + 1 - RING)
                passed()
                sp.dma_start(res[0:C, r, :], y_d[0][:, cols(w)]).then_inc(ring["y_in"][r], 16)
                pi, pr = step(i, r, -RING)
                if exists(NW, pi, pr):
                    sp.wait_ge(ring["table_written"][pr], 16 * rounds_of(NW, 2, pi, pr))
                    passed()
                sp.dma_start(xout[0:BLOCK, r, :, :], of_window(x, w)).then_inc(ring["x_in"][r], 16)

            over(sp, NW, load_last)

        @block.gpsimd
        def _(pool):
            made = Chain(pool, s["own_pool"])
            made.link(pool.memset(ident[:, :], 0.0))
            made.link(pool.memset(ones[:, :], 1.0))
            made.link(pool.memset(zeros[:, :], 0.0))
            made.link(pool.memset(ones_b[:, :], 1.0))
            made.link(pool.affine_select(out=ident[:, :], in_=ident[:, :], compare_op=ALU.not_equal, fill=1.0, base=0,
                                         pattern=[[-1, P]], channel_multiplier=1))
            made.link(pool.affine_select(out=lower[:, :], in_=ones[:, :], compare_op=ALU.is_gt, fill=0.0, base=0,
                                         pattern=[[-1, P]], channel_multiplier=1))
            made.link(pool.memset(wext[:, :, :], 0.0))
            made.link(pool.memset(wext[C:C + 1, :, C:C + 1], 1.0))
            made.link(pool.memset(minus[:, :], -1))
            made.link(pool.iota(iota_i[:, :], pattern=[[1, W]], base=0, channel_multiplier=0))
            made.link(pool.tensor_copy(iota[:, :], iota_i[:, :]))
            made.link(pool.memset(row_pen[0:1, CE:CE + 1], -BIG))
            made.link(pool.memset(Y[C:C + 1, :, :], 1.0))
            pool.sem_inc(s["consts_made"], 1)
            pool.memset(acc[:, :], 0.0).then_inc(s["acc_clear"], 1)
            last_node = pool.to_reg(N - 1)

            def fast(l):
                def turn(i, r):
                    q = l * NCH + i * RING + r
                    pool.wait_ge(s["idx_ready"], q + 1)
                    since(pool, "summed", q + 1 - RING)
                    pool.sem_inc(s["pool_passed"], 1)
                    for t in range(CT):
                        pool.indirect_dma_start(rows[:, r, t, :], None, table,
                                                bass.IndirectOffsetOnAxis(ap=c_idx[:, r, t:t + 1], axis=0)).then_inc(ring["gathered"][r], 16)

                over(pool, NCH, turn)
                for r in range(min(RING, NCH)):
                    pool.wait_ge(ring["gathered"][r], 16 * CT * len(range(r, NCH, RING)) * (l + 1))

            def general(l):
                pool.wait_ge(g[l]["gi_written"], 16 * NW)

                def tile(t):
                    pool.wait_ge(g[l]["e_src"], 16 * t + 16)
                    pool.wait_ge(g[l]["e_dst"], 16 * t + 16)
                    since(pool, g[l]["e_scattered"], 16 * t)
                    pool.sem_inc(s["pool_passed"], 1)
                    pool.indirect_dma_start(g_rows[:, :], None, table, bass.IndirectOffsetOnAxis(ap=g_src[:, 0:1], axis=0)).then_inc(g[l]["e_rows"], 16)
                    pool.indirect_dma_start(g_old[:, :], None, state, bass.IndirectOffsetOnAxis(ap=g_dst[:, 0:1], axis=0)).then_inc(g[l]["e_old"], 16)
                    pool.wait_ge(g[l]["e_new"], t + 1)
                    pool.sem_inc(s["pool_passed"], 1)
                    pool.indirect_dma_start(state, bass.IndirectOffsetOnAxis(ap=g_sidx[:, 0:1], axis=0), g_new[:, :], None,
                                            bounds_check=last_node, oob_is_err=False).then_inc(g[l]["e_scattered"], 16)

                tile(0)
                with pool.Fori(1, TILES) as t:
                    tile(t)
                pool.wait_ge(g[l]["e_scattered"], 16 * TILES)

            pool.wait_ge(s["flag_ready"], 1)
            unordered = pool.value_load(flag[0:1, 0:1], min_val=0, max_val=1)
            for l in range(2):
                all_landed(pool, "table_written", NW, l + 1)
                edges(pool, unordered, fast, general, l)

        @block.scalar
        def _(act):
            own = Chain(act, s["own_scalar"])

            COPY_LAG = 2

            def copy_table(l, i, r):
                if not exists(NW, i, r):
                    return
                w = i * RING + r
                act.wait_ge(s["projected"], l * NW + w + 1)
                last_rows(act, "table_written", l, i, r)
                act.activation(tabs[0:BLOCK, r, :, :], bank_rows[r][0:BLOCK, 0:BPW * ROW].rearrange("p (b c) -> p b c", b=BPW), ACT.Copy).then_inc(s["tab_copied"], 1)

            def last_rows(eng, name, l, i, r):
                pi, pr = step(i, r, -RING)
                if exists(NW, pi, pr):
                    eng.wait_ge(ring[name][pr], 16 * rounds_of(NW, l, pi, pr))

            def fast(l):
                own = Chain(act, own_sems["scalar", "fast", l])

                def indices(i, r):
                    if not exists(NCH, i, r):
                        return
                    q = l * NCH + i * RING + r
                    act.wait_ge(s["turned"], q + 1)
                    own.link(act.activation(c_dl[:, r, :, :], psT[:, CT:3 * CT].rearrange("p (k t) -> p k t", k=2), ACT.Copy))
                    act.activation(c_idx[:, r, :], psT[:, 0:CT], ACT.Copy).then_inc(s["idx_ready"], 1)

                def scale(i, r, k):
                    if not exists(NCH, i, r):
                        return
                    for t in range(k * GT, (k + 1) * GT):
                        last = act.activation(rows[:, r, t, 0:C + 1], rows[:, r, t, 0:C + 1], ACT.Copy, scale=c_w[:, PAIR[r], t:t + 1])
                    last.then_inc(s["scaled"], 1)

                def own_scores(i, r, k):
                    if not exists(NCH, i, r):
                        return
                    q = l * NCH + i * RING + r
                    n = min(TURNED, CT - k * TURNED)
                    act.wait_ge(s["onehot_turned"], q * TURNS + k + 1)
                    since(act, "own_psum", q * TURNS + last_use(k) + 1)
                    act.activation(onehot_t[0:W, k % TURN_BANKS, 0:n * P], bank_own[k % TURN_BANKS][0:W, 0:n * P], ACT.Copy).then_inc(s["onehot_copied"], 1)

                def turn(i, r):
                    q = l * NCH + i * RING + r
                    act.wait_ge(s["v_turned"], q + 1)
                    since(act, "vrow_in", 16 * q)
                    act.activation(t_v[0:CT, :], psH[0:CT, 0:P], ACT.Copy).then_inc(s["vt_ready"], 1)
                    indices(*step(i, r, 2))
                    for k in range(max(TURNS, GROUPS)):
                        if k < TURNS:
                            own_scores(*step(i, r, 1), k)
                        if k < GROUPS:
                            scale(*step(i, r, -1), k)
                    act.wait_ge(s["scored"], q + 1)
                    act.activation(fr[0:1, 3:4], fr[0:1, 2:3], ACT.Exp).then_inc(s["factor_ready"], 1)
                    own.link(act.activation(c_w[:, PAIR[r], :], c_s[:, 1, :], ACT.Exp))

                indices(0, 0)
                indices(0, 1)
                for k in range(TURNS):
                    own_scores(0, 0, k)
                over(act, NCH, turn, own, 2 * RING)
                for k in range(GROUPS):
                    scale((NCH - 1) // RING, (NCH - 1) % RING, k)

            def general(l):
                with act.Fori(0, TILES) as t:
                    act.wait_ge(g[l]["e_wt"], t + 1)
                    act.activation(g_c[:, 4:6], g_c[:, 2:4], ACT.Exp).then_inc(g[l]["e_exp"], 1)
                with act.Fori(0, NW) as w:
                    act.wait_ge(g[l]["gb_turned"], w + 1)
                    act.activation(acc[0:STATE - 1, cols(w)], psT[0:STATE - 1, 0:WIN], ACT.Copy).then_inc(g[l]["gb_copied"], 1)

            def finish(l):
                def bias(i, r):
                    if not exists(NW, i, r):
                        return
                    w = i * RING + r
                    act.wait_ge(s["norm_ready"], l * NW + w + 1)
                    act.activation(acc[0:C, cols(w)], acc[0:C, cols(w)], ACT.Identity, bias=gn[0:C, l:l + 1],
                                   accum_out=win_sum[0:C, 0, bass.ds(w, 1)]).then_inc(s["biased"], 1)

                def copy_weights(i, r):
                    if not exists(NW, i, r):
                        return
                    n = l * NW + i * RING + r
                    act.wait_ge(s["z_spread"], n + 1)
                    since(act, "norm_ready", n + 1 - RING)
                    act.activation(lin[0:C, r, :], bank_tab[PAIR[r]][0:C, 0:WIN], ACT.Copy).then_inc(s["z_copied"], 1)

                def turn(i, r):
                    copy_weights(*step(i, r, 3))
                    bias(*step(i, r, 1))
                    w = i * RING + r
                    act.wait_ge(s["biased"], l * NW + w + 1)
                    act.activation(junk[0:C, PAIR[r], :], acc[0:C, cols(w)], ACT.Square, bias=stat[0:C, 8:9],
                                   accum_out=win_sum[0:C, 1, bass.ds(w, 1)]).then_inc(s["square_ready"], 1)

                act.wait_ge(s["z_moved"], 32 * (l + 1))
                act.activation(z_col[0:BLOCK, 1, :], z_col[0:BLOCK, 1, :], ACT.Exp, scale=-1.0).then_inc(s["self_weight"], 1)
                for r in range(3):
                    copy_weights(0, r)
                bias(0, 0)
                act.wait_ge(s["biased"], l * NW + 1)
                own.link(act.activation(stat[0:C, 8:9], win_sum[0:C, 0, 0:1], ACT.Copy, scale=-1.0 / WIN))
                over(act, NW, turn)
                act.wait_ge(s["gn_var"], l + 1)
                act.activation(stat[0:C, 4:5], stat[0:C, 3:4], ACT.Sqrt).then_inc(s["gn_std"], 1)
                act.wait_ge(s["gn_ready"], l + 1)

            def affine(l, i, r):
                w = i * RING + r
                since(act, "y_ready" if l == 0 else "v_ready", (NW if l == 0 else 0) + w + 1 - RING)
                act.activation(lin[0:C, r, :], acc[0:C, cols(w)], ACT.Identity, bias=stat[0:C, 6:7], scale=stat[0:C, 5:6]).then_inc(s["lin_ready"], 1)

            for k, (w, n) in enumerate(x_loads):
                act.wait_ge(s["centred"], k + 1)
                since(act, "square_used", k - 1)
                at = (k % 2) * X_LOAD * BXW
                act.activation(squares[0:BLOCK, at:at + n * BXW], big[0:BLOCK, w * BXW:(w + n) * BXW], ACT.Square).then_inc(s["square_made"], 1)
            act.wait_ge(s["var_ready"], 1)
            act.activation(xs[0:BLOCK, 2, :], xs[0:BLOCK, 1, :], ACT.Sqrt).then_inc(s["std_ready"], 1)
            act.wait_ge(s["wt_psum"], 2)
            for l in range(2):
                act.activation(wext[0:C, l, 0:C], psT[0:C, l * C:(l + 1) * C], ACT.Copy).then_inc(s["wt_copied"], 1)
                act.activation(wext[0:C, l, C + 1:ROW], psT[0:C, 2 * C + 2 * l:2 * C + 2 * l + 2], ACT.Copy).then_inc(s["wt_copied"], 1)

            def first_turn(i, r):
                w = i * RING + r
                act.wait_ge(s["xt_done"], w + 1)
                since(act, "projected", w + 1 - RING)
                last_rows(act, "y_written", 0, i, r)
                act.activation(Y[0:C, r, :], bank_turn[PAIR[r]][0:C, 0:WIN], ACT.Copy).then_inc(s["y_ready"], 1)
                copy_table(0, *step(i, r, -COPY_LAG))

            over(act, NW, first_turn)
            for w in range(max(NW - COPY_LAG, 0), NW):
                copy_table(0, w // RING, w % RING)
            act.wait_ge(s["flag_ready"], 1)
            unordered = act.value_load(flag[0:1, 0:1], min_val=0, max_val=1)
            edges(act, unordered, fast, general, 0)
            finish(0)

            def second_turn(i, r):
                affine(0, i, r)
                copy_table(1, *step(i, r, -COPY_LAG))

            over(act, NW, second_turn)
            for w in range(max(NW - COPY_LAG, 0), NW):
                copy_table(1, w // RING, w % RING)
            edges(act, unordered, fast, general, 1)
            finish(1)
            OUT_LAG = 3

            def store_out(i, r):
                if not exists(NW, i, r):
                    return
                w = i * RING + r
                act.wait_ge(s["out_ready"], w + 1)
                act.sem_inc(s["act_passed"], 1)
                act.dma_start(of_window(out, w), xout[0:BLOCK, r, :, :]).then_inc(ring["table_written"][r], 16)

            def last_turn(i, r):
                affine(1, i, r)
                store_out(*step(i, r, -OUT_LAG))

            over(act, NW, last_turn)
            for w in range(max(NW - OUT_LAG, 0), NW):
                store_out(w // RING, w % RING)
            all_landed(act, "table_written", NW, 3)

        @block.tensor
        def _(pe):
            def passed():
                pe.sem_inc(s["pe_passed"], 1)

            pe.wait_ge(s["consts_made"], 1)
            pe.wait_ge(s["weights_in"], 16 * 11)
            for l in range(2):
                pe.transpose(psT[0:C, l * C:(l + 1) * C], wraw[0:C, l, :], ident[0:C, 0:C])
                pe.matmul(psT[0:C, 2 * C + 2 * l:2 * C + 2 * l + 2], wraw[0:C, l, :], avec[0:C, 2 * l:2 * l + 2], start=True, stop=True).then_inc(s["wt_psum"], 1)
            pe.wait_ge(s["wt_copied"], 4)

            def project(l, i, r):
                if not exists(NW, i, r):
                    return
                n = l * NW + i * RING + r
                pe.wait_ge(s["y_ready"], n + 1)
                since(pe, "tab_copied", n + 1 - RING)
                for b in range(BPW):
                    last = pe.matmul(bank_rows[r][0:BLOCK, b * ROW:(b + 1) * ROW], Y[0:C + 1, r, b:WIN:BPW], wext[0:C + 1, l, :], start=True, stop=True)
                last.then_inc(s["projected"], 1)

            def fast(l):
                def turn_indices(i, r):
                    if not exists(NCH, i, r):
                        return
                    q = l * NCH + i * RING + r
                    pe.wait_ge(s["prep_made"], q + 1)
                    since(pe, "idx_ready", q)
                    since(pe, "own_ready", q - 1)
                    passed()
                    for k in range(3):
                        last = pe.transpose(psT[:, k * CT:(k + 1) * CT], t_flt[0:CT, r, k, :], ident[0:CT, 0:CT])
                    last.then_inc(s["turned"], 1)

                def turn_onehot(i, r, k):
                    if not exists(NCH, i, r):
                        return
                    q = l * NCH + i * RING + r
                    pe.wait_ge(s["expanded"], q + 1)
                    since(pe, "onehot_copied", q * TURNS + last_use(k) + 1)
                    passed()
                    for t in range(k * TURNED, min((k + 1) * TURNED, CT)):
                        last = pe.transpose(bank_own[k % TURN_BANKS][0:W, (t % TURNED) * P:(t % TURNED + 1) * P], onehot[:, r, t, :], ident[:, :])
                    last.then_inc(s["onehot_turned"], 1)

                def choose(i, r, k):
                    if not exists(NCH, i, r):
                        return
                    q = l * NCH + i * RING + r
                    if k == 0:
                        pe.wait_ge(s["awin_split"], q + 1)
                        for n in (1, 0):
                            if exists(NCH, *step(i, r, n)):
                                pe.wait_ge(s["idx_ready"], q + n + 1)
                                break
                    pe.wait_ge(s["onehot_copied"], q * TURNS + k + 1)
                    passed()
                    for t in range(k * TURNED, min((k + 1) * TURNED, CT)):
                        at = 3 * CT + t * PARTS * 2
                        last = pe.matmul(psT[:, at:at + PARTS * 2], onehot_t[0:W, k % TURN_BANKS, (t % TURNED) * P:(t % TURNED + 1) * P],
                                         a_parts[0:W, r, t // GT, :, :].rearrange("p s k -> p (s k)"), start=True, stop=True)
                    last.then_inc(s["own_psum"], 1)

                def sum_windows(i, r, k):
                    if not exists(NCH, i, r):
                        return
                    q = l * NCH + i * RING + r
                    if k == 0:
                        since(pe, "added", q - 1)
                        pe.wait_ge(s["factor_ready"], q + 1)
                        pe.matmul(bank_sum[PAIR[r]][0:C + 1, FACTOR:FACTOR + 1], ones[0:1, 0:C + 1], fr[0:1, 3:4], start=True, stop=True)
                    pe.wait_ge(s["scaled"], GROUPS * q + k + 1)
                    for t in range(k * GT, (k + 1) * GT):
                        last = pe.matmul(bank_sum[PAIR[r]][0:SUMS, k * W:(k + 1) * W], rows[:, r, t, 0:SUMS], onehot[:, r, t, :],
                                         start=(t % GT == 0), stop=(t % GT == GT - 1))
                    if k == GROUPS - 1:
                        last.then_inc(s["summed"], 1)

                def turn(i, r):
                    q = l * NCH + i * RING + r
                    after, before = step(i, r, 1), step(i, r, -1)
                    pe.wait_ge(s["v_col"], q + 1)
                    since(pe, "vt_ready", q)
                    pe.transpose(psH[0:CT, 0:P], c_v[:, :], ident[:, :]).then_inc(s["v_turned"], 1)
                    turn_indices(*step(i, r, 2))
                    for k in range(max(TURNS, GROUPS) + 1):
                        if k < TURNS:
                            turn_onehot(*after, k)
                        if 0 < k <= TURNS:
                            choose(*after, k - 1)
                        if 0 < k <= GROUPS:
                            sum_windows(*before, k - 1)
                        if k == M_TURN:
                            pe.wait_ge(s["mrow_back"], 16 * (q + 1))
                            since(pe, "scored", q)
                            passed()
                            pe.transpose(psTab[:, 0:CT], t_m[0:CT, :], ident[0:CT, 0:CT]).then_inc(s["m_turned"], 1)

                turn_indices(0, 0)
                turn_indices(0, 1)
                for k in range(TURNS):
                    turn_onehot(0, 0, k)
                    if k > 0:
                        choose(0, 0, k - 1)
                choose(0, 0, TURNS - 1)
                over(pe, NCH, turn)
                for k in range(GROUPS):
                    sum_windows((NCH - 1) // RING, (NCH - 1) % RING, k)

            def general(l):
                with pe.Fori(0, TILES) as t:
                    pe.wait_ge(g[l]["e_diag"], t + 1)
                    pe.matmul(psE[:, 0:P], ones[:, :], g_diag[:, :], start=True, stop=True).then_inc(g[l]["e_row"], 1)
                    pe.wait_ge(g[l]["e_weighted"], t + 1)
                    pe.matmul(psU[:, 0:C + 1], g_eq[:, :], g_w[:, 0:C + 1], start=True, stop=True).then_inc(g[l]["e_sum"], 1)

                def turn_state(w):
                    pe.wait_ge(g[l]["gb_ready"], w + 1)
                    since(pe, g[l]["gb_copied"], w)
                    for b in range(BPW):
                        last = pe.transpose(psT[0:STATE, b:WIN:BPW], g_init[0:BLOCK, b, :], ident[0:BLOCK, 0:BLOCK])
                    last.then_inc(g[l]["gb_turned"], 1)

                turn_state(0)
                with pe.Fori(1, NW) as w:
                    turn_state(w)
                pe.wait_ge(g[l]["gb_copied"], NW)

            def finish(l):
                def turn(i, r):
                    w = i * RING + r
                    n = l * NW + w
                    since(pe, "z_copied", n - 1)
                    pe.matmul(bank_tab[PAIR[r]][0:C, 0:WIN], ones_b[0:PARTS, 0:C], z_rows[0:PARTS, 1, cols(w)], start=True, stop=True).then_inc(s["z_spread"], 1)
                    pe.wait_ge(ring["y_in"][r], 16 * rounds_of(NW, l, i, r))
                    since(pe, "both_made", 2 * (n - 1))
                    pe.matmul(bank_turn[PAIR[r]][0:C, 0:WIN], wext[0:C, l, 0:C], Y[0:C, r, :], start=True, stop=True)
                    pe.matmul(bank_z[PAIR[r]][0:C, 0:WIN], ones_b[0:PARTS, 0:C], z_rows[0:PARTS, 0, cols(w)], start=True, stop=True).then_inc(s["h_spread"], 1)

                pe.wait_ge(s["edges_done"], l + 1)
                pe.wait_ge(s["z_back"], 32 * PARTS * (l + 1))
                over(pe, NW, turn)

            def first_turn(i, r):
                w = i * RING + r
                pe.wait_ge(s["xn_ready"], w + 1)
                since(pe, "y_ready", w + 1 - 2)
                for b in range(BPW):
                    last = pe.transpose(bank_turn[PAIR[r]][0:C, b:WIN:BPW], xn[0:BLOCK, r, b, :], ident[0:BLOCK, 0:BLOCK])
                last.then_inc(s["xt_done"], 1)
                project(0, *step(i, r, -1))

            over(pe, NW, first_turn)
            project(0, (NW - 1) // RING, (NW - 1) % RING)
            pe.wait_ge(s["tab_copied"], NW)
            pe.wait_ge(s["first_row"], 1)
            for at in range(0, NG, 512):
                width = min(512, NG - at)
                last = pe.matmul([psD, psZ][at // 512][:, 0:width], ones[0:1, :], first_f[0:1, at:at + width], start=True, stop=True)
            last.then_inc(s["first_spread"], 1)
            pe.wait_ge(s["check_done"], 1)
            pe.matmul(psE[0:1, 0:1], viol[0:NCH, 0:1], ones[0:NCH, 0:1], start=True, stop=True).then_inc(s["flag_psum"], 1)
            pe.wait_ge(s["flag_ready"], 1)
            unordered = pe.value_load(flag[0:1, 0:1], min_val=0, max_val=1)
            edges(pe, unordered, fast, general, 0)
            finish(0)
            over(pe, NW, lambda i, r: project(1, i, r))
            edges(pe, unordered, fast, general, 1)
            finish(1)

            def last_turn(i, r):
                w = i * RING + r
                pe.wait_ge(s["v_ready"], w + 1)
                since(pe, "out_ready", w + 1 - 2)
                for b in range(BPW):
                    last = pe.transpose(bank_tab[PAIR[r]][0:BLOCK, b * C:(b + 1) * C], Y[0:C, r, b:WIN:BPW], ident[0:C, 0:C])
                last.then_inc(s["v_back"], 1)

            over(pe, NW, last_turn)

        @block.vector
        def _(dve):
            own = Chain(dve, s["own_vector"])
            link = own.link

            def split_in_parts(link, parts, whole, rest):
                link(dve.tensor_copy(parts[:, 0], whole))
                link(dve.tensor_tensor(rest, whole, parts[:, 0], ALU.subtract))
                link(dve.tensor_copy(parts[:, 1], rest))
                link(dve.tensor_tensor(parts[:, 2], rest, parts[:, 1], ALU.subtract))

            def fast(l):
                own = Chain(dve, own_sems["vector", "fast", l])
                link = own.link

                def prepare(i, r):
                    if not exists(NCH, i, r):
                        return
                    q = l * NCH + i * RING + r
                    b = r
                    dve.wait_ge(s["prep_in"], 64 * (q + 1))
                    since(dve, "turned", q + 1 - RING)
                    since(dve, "penrow_in", 16 * (q + 1 - RING))
                    own.start(dve.tensor_tensor(t_pen[0:CT, b, :], t_int[0:CT, b, 1, :], t_int[0:CT, b, 2, :], ALU.is_equal))
                    dve.tensor_tensor(t_flt[0:CT, b, 2, :], t_int[0:CT, b, 1, :], t_int[0:CT, b, 3, :], ALU.not_equal)
                    own.settle()
                    link(dve.tensor_scalar(t_pen[0:CT, b, :], t_pen[0:CT, b, :], -1.0, BIG, ALU.add, ALU.mult))
                    dve.tensor_copy(t_flt[0:CT, b, 0:2, :], t_int[0:CT, b, 0:2, :]).then_inc(s["prep_made"], 1)

                def localise(i, r):
                    if not exists(NCH, i, r):
                        return
                    c = i * RING + r
                    dve.wait_ge(s["idx_ready"], l * NCH + c + 1)
                    by_group = c_dl[:, r, 0, :].rearrange("p (g t) -> p g t", g=GROUPS)
                    dve.tensor_tensor(by_group, by_group, first_all[:, bass.ds(c * GROUPS, GROUPS)].unsqueeze(2).to_broadcast([P, GROUPS, GT]),
                                      ALU.subtract).then_inc(s["dl_ready"], 1)

                def expand(i, r):
                    if not exists(NCH, i, r):
                        return
                    q = l * NCH + i * RING + r
                    since(dve, "summed", q + 1 - RING)
                    dve.wait_ge(s["dl_ready"], q + 1)
                    dve.tensor_tensor(onehot[:, r, :, :], iota[:, :].unsqueeze(1).to_broadcast([P, CT, W]),
                                      c_dl[:, r, 0, :].unsqueeze(2).to_broadcast([P, CT, W]), ALU.is_equal).then_inc(s["expanded"], 1)

                def split_windows(i, r):
                    if not exists(NCH, i, r):
                        return
                    dve.wait_ge(ring["awin_in"][r], 16 * GROUPS * rounds_of(NCH, l, i, r))
                    split_in_parts(link, a_parts[0:W, r, :, :, :].rearrange("p g s k -> p s g k"), a_win[0:W, r, :, :], a_rest[0:W, :, :])
                    dve.sem_inc(s["awin_split"], 1)

                def add_windows(i, r, starts):
                    if not exists(NCH, i, r):
                        return
                    q = l * NCH + i * RING + r
                    dve.wait_ge(s["summed"], q + 1)
                    for k, first in enumerate(starts):
                        if k == 0:
                            link(dve.tensor_tensor(acc[0:C + 1, bass.ds(first, 1)], acc[0:C + 1, bass.ds(first, 1)], bank_sum[PAIR[r]][0:C + 1, FACTOR:FACTOR + 1], ALU.mult))
                        link(dve.tensor_tensor(acc[0:SUMS, bass.ds(first, W)], acc[0:SUMS, bass.ds(first, W)],
                                               bank_sum[PAIR[r]][0:SUMS, k * W:(k + 1) * W], ALU.add))
                    dve.sem_inc(s["added"], 1)

                def turn(i, r):
                    q = l * NCH + i * RING + r
                    before = step(i, r, -1)
                    dve.wait_ge(ring["gathered"][r], 16 * CT * rounds_of(NCH, l, i, r))
                    dve.wait_ge(s["own_psum"], (q + 1) * TURNS)
                    chosen = psT[:, 3 * CT:(3 + 2 * PARTS) * CT].rearrange("p (t s k) -> p t k s", s=PARTS, k=2)
                    link(dve.tensor_reduce(c_own[:, r, :, :], chosen, AX, ALU.add))
                    dve.sem_inc(s["own_ready"], 1)
                    dve.tensor_tensor(c_v[:, :], rows[:, r, :, C + 1], c_own[:, r, :, 0], ALU.max).then_inc(s["v_col"], 1)
                    prepare(*step(i, r, 2))
                    localise(*step(i, r, 2))
                    link(dve.tensor_copy(fr[0:1, 0:1], carry[0:1, :]))
                    dve.wait_ge(s["vrow_in"], 16 * (q + 1))
                    dve.wait_ge(s["penrow_in"], 16 * (q + 1))
                    own.start(dve.tensor_tensor_scan(row_v[0:1, :], row_pen[0:1, 0:CE], row_v[0:1, :], carry[0:1, 0:1], ALU.add, ALU.max))
                    starts = window_starts(mybir.EngineType.DVE, before[0] * RING + before[1]) if exists(NCH, *before) else None
                    own.settle()
                    link(dve.tensor_tensor_scan(row_v[0:1, ::-1], row_pen[0:1, CE:0:-1], row_v[0:1, ::-1], -BIG, ALU.add, ALU.max))
                    own.start(dve.tensor_copy(carry[0:1, :], row_v[0:1, CE - 1:CE]))
                    link(dve.tensor_copy(fr[0:1, 1:2], row_v[0:1, 0:1]))
                    dve.sem_inc(s["scanned"], 1)
                    expand(*step(i, r, 2))
                    dve.tensor_tensor(c_q[:, 0, :], rows[:, r, :, C + 1], c_own[:, r, :, 1], ALU.add)
                    dve.tensor_tensor(c_q[:, 2, :], c_own[:, r, :, 0], c_own[:, r, :, 1], ALU.add)
                    link(dve.tensor_tensor(fr[0:1, 0:2], fr[0:1, 0:2], c_own[0:1, r, 0, 1:2].to_broadcast([1, 2]), ALU.add))
                    link(dve.scalar_tensor_tensor(out=fr[0:1, 0:2], in0=fr[0:1, 0:2], scalar=SLOPE_ATT, in1=fr[0:1, 0:2], op0=ALU.mult, op1=ALU.max))
                    own.start(dve.tensor_scalar(fr[0:1, 2:3], fr[0:1, 0:1], fr[0:1, 1:2], 0.0, ALU.subtract, ALU.min))
                    dve.wait_ge(s["m_turned"], q + 1)
                    link(dve.tensor_tensor(c_q[:, 1, :], psTab[:, 0:CT], c_own[:, r, :, 1], ALU.add))
                    link(dve.scalar_tensor_tensor(out=c_q[:, :, :], in0=c_q[:, :, :], scalar=SLOPE_ATT, in1=c_q[:, :, :], op0=ALU.mult, op1=ALU.max))
                    own.start(dve.tensor_tensor(c_s[:, 0, :], c_q[:, 1, :], c_q[:, 2, :], ALU.subtract))
                    dve.tensor_tensor(c_s[:, 1, :], c_q[:, 0, :], c_q[:, 1, :], ALU.subtract)
                    own.settle()
                    dve.tensor_tensor(rows[:, r, :, C + 1], c_s[:, 0, :], c_dl[:, r, 1, :], ALU.mult).then_inc(s["scored"], 1)
                    split_windows(*step(i, r, 2))
                    add_windows(*before, starts)

                link(dve.memset(carry[0:1, :], -BIG))
                for r in range(2):
                    prepare(0, r)
                for r in range(2):
                    localise(0, r)
                all_landed(dve, "table_written", NW, l + 1)
                all_landed(dve, "y_written", NW, l + 1)
                for r in range(2):
                    expand(0, r)
                    split_windows(0, r)
                over(dve, NCH, turn, own, 24 * RING)
                last = (NCH - 1) // RING, (NCH - 1) % RING
                add_windows(*last, window_starts(mybir.EngineType.DVE, NCH - 1))
                dve.sem_inc(s["edges_done"], 1)

            def general(l):
                own = Chain(dve, own_sems["vector", "general", l])
                link = own.link
                def make_state(w):
                    dve.wait_ge(g[l]["gi_in"], 16 * w + 16)
                    link(dve.tensor_tensor(g_alph[0:BLOCK, :], g_init[0:BLOCK, :, C + 1], g_init[0:BLOCK, :, C + 2], ALU.add))
                    dve.scalar_tensor_tensor(out=g_init[0:BLOCK, :, C + 1], in0=g_alph[0:BLOCK, :], scalar=SLOPE_ATT, in1=g_alph[0:BLOCK, :],
                                             op0=ALU.mult, op1=ALU.max).then_inc(g[l]["gi_ready"], 1)

                make_state(0)
                with dve.Fori(1, NW) as w:
                    own.enter(w - 1, 1)
                    make_state(w)
                own.leave(NW - 1)
                def tile(t):
                    dve.wait_ge(g[l]["e_dst"], 16 * t + 16)
                    dve.wait_ge(g[l]["e_dstrow"], 16 * t + 16)
                    since(dve, g[l]["e_scattered"], 16 * t)
                    link(dve.tensor_copy(g_c[:, 0:1], g_dst[:, :]))
                    link(dve.tensor_copy(g_tmp[:, :], g_dstrow[:, :]))
                    link(dve.tensor_scalar(g_eq[:, :], g_tmp[:, :], g_c[:, 0:1], None, ALU.is_equal))
                    link(dve.tensor_tensor(g_tmp[:, :], g_eq[:, :], lower[:, :], ALU.mult))
                    link(dve.tensor_reduce(g_c[:, 1:2], g_tmp[:, :], AX, ALU.add))
                    dve.scalar_tensor_tensor(out=g_sidx[:, :], in0=g_c[:, 1:2], scalar=1e6, in1=g_c[:, 0:1], op0=ALU.mult, op1=ALU.add)
                    dve.wait_ge(g[l]["e_rows"], 16 * t + 16)
                    dve.wait_ge(g[l]["e_old"], 16 * t + 16)
                    link(dve.tensor_tensor(g_c[:, 6:7], g_rows[:, C + 1:C + 2], g_old[:, C + 2:C + 3], ALU.add))
                    link(dve.scalar_tensor_tensor(out=g_c[:, 1:2], in0=g_c[:, 6:7], scalar=SLOPE_ATT, in1=g_c[:, 6:7], op0=ALU.mult, op1=ALU.max))
                    dve.tensor_scalar(g_diag[:, :], ident[:, :], g_c[:, 1:2], None, ALU.mult).then_inc(g[l]["e_diag"], 1)
                    link(dve.tensor_scalar(g_tmp[:, :], g_eq[:, :], BIG, -BIG, ALU.mult, ALU.add))
                    dve.wait_ge(g[l]["e_row"], t + 1)
                    link(dve.tensor_tensor(g_tmp[:, :], g_tmp[:, :], psE[:, 0:P], ALU.add))
                    link(dve.tensor_reduce(g_c[:, 6:7], g_tmp[:, :], AX, ALU.max))
                    link(dve.tensor_tensor(g_new[:, C + 1:C + 2], g_c[:, 6:7], g_old[:, C + 1:C + 2], ALU.max))
                    dve.tensor_tensor(g_c[:, 2:3], g_old[:, C + 1:C + 2], g_new[:, C + 1:C + 2], ALU.subtract)
                    link(dve.tensor_tensor(g_c[:, 3:4], g_c[:, 1:2], g_new[:, C + 1:C + 2], ALU.subtract))
                    dve.tensor_copy(g_new[:, C + 2:C + 3], g_old[:, C + 2:C + 3]).then_inc(g[l]["e_wt"], 1)
                    dve.wait_ge(g[l]["e_exp"], t + 1)
                    dve.tensor_scalar(g_w[:, 0:C + 1], g_rows[:, 0:C + 1], g_c[:, 5:6], None, ALU.mult).then_inc(g[l]["e_weighted"], 1)
                    dve.wait_ge(g[l]["e_sum"], t + 1)
                    dve.scalar_tensor_tensor(out=g_new[:, 0:C + 1], in0=g_old[:, 0:C + 1], scalar=g_c[:, 4:5], in1=psU[:, 0:C + 1],
                                             op0=ALU.mult, op1=ALU.add).then_inc(g[l]["e_new"], 1)

                tile(0)
                with dve.Fori(1, TILES) as t:
                    own.enter(t - 1, 12)
                    tile(t)
                own.leave(TILES - 1)
                with dve.Fori(0, NW) as w:
                    dve.wait_ge(g[l]["gb_in"], 16 * w + 16)
                    dve.memset(g_init[0:BLOCK, :, C + 1:C + 2], 1e4).then_inc(g[l]["gb_ready"], 1)
                dve.wait_ge(g[l]["gb_copied"], NW)
                dve.sem_inc(s["edges_done"], 1)

            def finish(l):
                def add(i, r):
                    if not exists(NW, i, r):
                        return
                    w = i * RING + r
                    dve.wait_ge(s["both_made"], 2 * (l * NW + w + 1))
                    dve.tensor_tensor(acc[0:C, cols(w)], acc[0:C, cols(w)], lin[0:C, r, :], ALU.add).then_inc(s["norm_ready"], 1)

                def turn(i, r):
                    w = i * RING + r
                    dve.wait_ge(s["h_spread"], l * NW + w + 1)
                    dve.wait_ge(s["z_copied"], l * NW + w + 1)
                    dve.tensor_tensor(lin[0:C, r, :], lin[0:C, r, :], bank_turn[PAIR[r]][0:C, 0:WIN], ALU.mult).then_inc(s["both_made"], 1)
                    add(*step(i, r, -1))
                    dve.tensor_tensor(acc[0:C, cols(w)], acc[0:C, cols(w)], bank_z[PAIR[r]][0:C, 0:WIN], ALU.mult).then_inc(s["both_made"], 1)

                link(dve.memset(Y[C:C + 1, :, :], 1.0))
                dve.wait_ge(s["self_weight"], l + 1)
                link(dve.tensor_tensor(z_rest[0:BLOCK, 0, :], z_col[0:BLOCK, 0, :], z_col[0:BLOCK, 1, :], ALU.add))
                link(dve.reciprocal(z_col[0:BLOCK, 0, :], z_rest[0:BLOCK, 0, :]))
                link(dve.tensor_tensor(z_col[0:BLOCK, 1, :], z_col[0:BLOCK, 1, :], z_col[0:BLOCK, 0, :], ALU.mult))
                split_in_parts(link, z_parts[0:BLOCK, :, :, :], z_col[0:BLOCK, :, :], z_rest[0:BLOCK, :, :])
                dve.sem_inc(s["z_split"], 1)
                over(dve, NW, turn)
                add((NW - 1) // RING, (NW - 1) % RING)
                dve.wait_ge(s["square_ready"], NW * (l + 1))
                link(dve.tensor_reduce(stat[0:C, 0:1], win_sum[0:C, 0, :], AX, ALU.add))
                link(dve.tensor_reduce(stat[0:C, 2:3], win_sum[0:C, 1, :], AX, ALU.add))
                link(dve.tensor_scalar(stat[0:C, 7:8], stat[0:C, 0:1], -1.0 / N, None, ALU.mult))
                link(dve.tensor_tensor(stat[0:C, 1:2], stat[0:C, 7:8], gn[0:C, 4:5], ALU.mult))
                link(dve.tensor_tensor(stat[0:C, 9:10], stat[0:C, 1:2], stat[0:C, 8:9], ALU.subtract))
                link(dve.tensor_tensor(stat[0:C, 10:11], stat[0:C, 8:9], stat[0:C, 7:8], ALU.subtract))
                link(dve.scalar_tensor_tensor(out=stat[0:C, 11:12], in0=stat[0:C, 10:11], scalar=2.0, in1=stat[0:C, 9:10], op0=ALU.mult, op1=ALU.add))
                link(dve.tensor_tensor(stat[0:C, 10:11], stat[0:C, 11:12], stat[0:C, 9:10], ALU.mult))
                link(dve.scalar_tensor_tensor(out=stat[0:C, 11:12], in0=stat[0:C, 2:3], scalar=1.0 / N, in1=stat[0:C, 10:11], op0=ALU.mult, op1=ALU.add))
                dve.tensor_scalar(stat[0:C, 3:4], stat[0:C, 11:12], EPS, None, ALU.add).then_inc(s["gn_var"], 1)
                dve.wait_ge(s["gn_std"], l + 1)
                link(dve.reciprocal(stat[0:C, 7:8], stat[0:C, 4:5]))
                link(dve.tensor_tensor(stat[0:C, 5:6], stat[0:C, 7:8], gn[0:C, 2:3], ALU.mult))
                link(dve.tensor_tensor(stat[0:C, 7:8], stat[0:C, 5:6], stat[0:C, 1:2], ALU.mult))
                dve.tensor_tensor(stat[0:C, 6:7], stat[0:C, 7:8], gn[0:C, 3:4], ALU.add).then_inc(s["gn_ready"], 1)

            def variance(k):
                w, n = x_loads[k]
                blocks = slice(w * BPW, (w + n) * BPW)
                at = (k % 2) * X_LOAD * BXW
                dve.wait_ge(s["square_made"], k + 1)
                link(dve.tensor_reduce(xs[0:BLOCK, 0, blocks], squares[0:BLOCK, at:at + n * BXW].rearrange("p (b c) -> p b c", c=C), AX, ALU.add))
                dve.sem_inc(s["square_used"], 1)

            for k, (w, n) in enumerate(x_loads):
                blocks = slice(w * BPW, (w + n) * BPW)
                xw = big[0:BLOCK, w * BXW:(w + n) * BXW].rearrange("p (b c) -> p b c", c=C)
                dve.wait_ge(x_loaded[k], 16)
                link(dve.tensor_reduce(xs[0:BLOCK, 3, blocks], xw, AX, ALU.add))
                link(dve.tensor_scalar(xs[0:BLOCK, 3, blocks], xs[0:BLOCK, 3, blocks], 1.0 / C, None, ALU.mult))
                dve.tensor_tensor(xw, xw, xs[0:BLOCK, 3, blocks].unsqueeze(2).to_broadcast([BLOCK, n * BPW, C]), ALU.subtract).then_inc(s["centred"], 1)
                if k > 0:
                    variance(k - 1)
            variance(len(x_loads) - 1)
            dve.tensor_scalar(xs[0:BLOCK, 1, :], xs[0:BLOCK, 0, :], 1.0 / C, EPS, ALU.mult, ALU.add).then_inc(s["var_ready"], 1)
            dve.wait_ge(s["std_ready"], 1)
            link(dve.reciprocal(xs[0:BLOCK, 3, :], xs[0:BLOCK, 2, :]))

            def first_turn(i, r):
                w = i * RING + r
                since(dve, "xt_done", w + 1 - RING)
                dve.scalar_tensor_tensor(out=xn[0:BLOCK, r, :, :], in0=big[0:BLOCK, bass.ds(w * BXW, BXW)].rearrange("p (b c) -> p b c", c=C), scalar=0.0,
                                         in1=xs[0:BLOCK, 3, bass.ds(w * BPW, BPW)].unsqueeze(2).to_broadcast([BLOCK, BPW, C]), op0=ALU.max, op1=ALU.mult).then_inc(s["xn_ready"], 1)

            over(dve, NW, first_turn)
            dve.wait_ge(s["firsts_in"], 32)
            dve.tensor_copy(last_f[0:1, :], last_i[0:1, :])
            link(dve.tensor_copy(first_f[0:1, :], first_i[0:1, :]))
            dve.sem_inc(s["first_row"], 1)
            link(dve.tensor_tensor(last_f[0:1, :], last_f[0:1, :], first_f[0:1, :], ALU.subtract))
            link(dve.tensor_scalar(last_f[0:1, :], last_f[0:1, :], float(W), None, ALU.is_ge))
            link(dve.tensor_reduce(viol[0:1, 1:2], last_f[0:1, :], AX, ALU.add))
            dve.wait_ge(s["check_in"], 32)
            link(dve.tensor_tensor(row_v[0:NCH, :], row_v[0:NCH, :].bitcast(I32), row_pen[0:NCH, 0:CE].bitcast(I32), ALU.is_gt))
            link(dve.tensor_reduce(viol[0:NCH, 0:1], row_v[0:NCH, :], AX, ALU.add))
            dve.sem_inc(s["check_done"], 1)
            dve.wait_ge(s["flag_psum"], 1)
            link(dve.tensor_tensor(viol[0:1, 2:3], psE[0:1, 0:1], viol[0:1, 1:2], ALU.add))
            link(dve.tensor_scalar(flag[0:1, :], viol[0:1, 2:3], 0.5, None, ALU.is_ge))
            dve.sem_inc(s["flag_ready"], 1)
            dve.wait_ge(s["first_spread"], 1)
            for at in range(0, NG, 512):
                width = min(512, NG - at)
                link(dve.tensor_copy(first_all[:, at:at + width], [psD, psZ][at // 512][:, 0:width]))
            dve.wait_ge(s["acc_clear"], 1)
            unordered = dve.value_load(flag[0:1, 0:1], min_val=0, max_val=1)
            edges(dve, unordered, fast, general, 0)
            finish(0)

            def second_turn(i, r):
                w = i * RING + r
                dve.wait_ge(s["lin_ready"], w + 1)
                d = RING
                if exists(NW, *step(i, r, -d)):
                    dve.wait_ge(s["projected"], NW + w + 1 - d)
                    pi, pr = step(i, r, -d)
                    dve.wait_ge(ring["y_written"][pr], 16 * rounds_of(NW, 1, pi, pr))
                dve.scalar_tensor_tensor(out=Y[0:C, r, :], in0=lin[0:C, r, :], scalar=SLOPE_ACT, in1=lin[0:C, r, :],
                                         op0=ALU.mult, op1=ALU.max).then_inc(s["y_ready"], 1)
                dve.tensor_scalar(acc[0:SUMS, cols(w)], ident[0:SUMS, 0:1].to_broadcast([SUMS, WIN]), 0.0, None, ALU.mult)

            over(dve, NW, second_turn)
            edges(dve, unordered, fast, general, 1)
            finish(1)

            def last_turn(i, r):
                w = i * RING + r
                dve.wait_ge(s["lin_ready"], w + NW + 1)
                dve.wait_ge(ring["y_in"][r], 16 * rounds_of(NW, 2, i, r))
                link(dve.tensor_tensor(res[0:C, r, :], lin[0:C, r, :], res[0:C, r, :], ALU.add))
                since(dve, "v_back", w + 1 - RING)
                dve.scalar_tensor_tensor(out=Y[0:C, r, :], in0=res[0:C, r, :], scalar=SLOPE_ACT, in1=res[0:C, r, :],
                                         op0=ALU.mult, op1=ALU.max).then_inc(s["v_ready"], 1)
                add_x(*step(i, r, -1))

            def add_x(i, r):
                if not exists(NW, i, r):
                    return
                dve.wait_ge(s["v_back"], i * RING + r + 1)
                dve.wait_ge(ring["x_in"][r], 16 * rounds_of(NW, 0, i, r))
                dve.tensor_tensor(xout[0:BLOCK, r, :, :], bank_tab[PAIR[r]][0:BLOCK, 0:BXW].rearrange("p (b c) -> p b c", b=BPW),
                                  xout[0:BLOCK, r, :, :], ALU.add).then_inc(s["out_ready"], 1)

            over(dve, NW, last_turn, own, RING)
            add_x((NW - 1) // RING, (NW - 1) % RING)


_INS = ["x", "src", "dst", "L0_gnn_W1", "L0_gnn_att_src1", "L0_gnn_att_dst1", "L0_gnn_b1", "L0_gnn_W2", "L0_gnn_att_src2",
        "L0_gnn_att_dst2", "L0_gnn_b2", "L0_gnn_gn_weight", "L0_gnn_gn_bias", "L0_gnn_gn_mean_scale"]


def kernel(**inputs):
    import numpy as _np
    import concourse.bacc as _bacc
    from concourse import mybir as _mybir
    from concourse.bass_utils import run_bass_kernel_spmd as _run

    nc = _bacc.Bacc("TRN2", target_bir_lowering=False, num_devices=1)
    arrays, args = {}, []
    for name in _INS:
        a = _np.ascontiguousarray(inputs[name])
        arrays[f"in_{name}_dram"] = a
        args.append(nc.dram_tensor(f"in_{name}_dram", a.shape, _mybir.dt.from_np(a.dtype), kind="ExternalInput").ap())
    args.append(nc.dram_tensor("out_0_dram", inputs["x"].shape, _mybir.dt.float32, kind="ExternalOutput").ap())
    gat_kernel(nc, *args)
    r = _run(nc, [arrays], core_ids=[0])
    return r.results[0]["out_0_dram"]
```
